# Optimizing a Trainium2 kernel written in Bass

```python
import numpy as np
import jax
import jax.numpy as jnp

def _softmax(x, axis=-1):
    return jax.nn.softmax(x, axis=axis)
def _gelu(x):
    return jax.nn.gelu(x, approximate=True)
def _silu(x):
    return jax.nn.silu(x)
def _sigmoid(x):
    return jax.nn.sigmoid(x)
def _layernorm(x, axis=-1, eps=1e-5):
    m = jnp.mean(x, axis=axis, keepdims=True)
    v = jnp.var(x, axis=axis, keepdims=True)
    return (x - m) / jnp.sqrt(v + eps)
def _scatter_add(tgt, idx, src, axis=0):
    return tgt.at[idx].add(src)
def _segment_sum(src, seg, n):
    return jax.ops.segment_sum(src, seg, n)

kernel_name = 'mk_adj_resnorm_d4_adj_256_d1b5c1'

def setup_inputs(seed: int = 0):
    np.random.seed(seed)
    _w = jnp.asarray
    def _rec_inputs():
        import jax
        import jax.numpy as jnp
        _gk = jax.random.key(seed)
        x = -0.0002928 + 1 * jax.random.normal(jax.random.fold_in(_gk, 1), (32, 512, 256), jnp.float32)
        _w = (1.0 + jnp.arange(512, dtype=jnp.float32)) ** -0.5
        _w = _w / _w.mean()
        _pij = jnp.clip(0.015625 * _w[:, None] * _w[None, :], 0.0, 1.0)
        _a = jax.random.uniform(jax.random.fold_in(_gk, 2), (512, 512)) < _pij
        adj = _a.astype(jnp.int32)
        return x, adj
    x, adj = _rec_inputs()
    def _L0_gnn_setup():
        import jax, jax.numpy as jnp
        import numpy as np
        NEG_BIG = -9000000000000000.0
        key = jax.random.key(seed)
        k1, k2, k3, k4 = jax.random.split(key, 4)
        bs, N, Fin, Fout = (8, 2048, 256, 256)
        x = jax.random.normal(k1, (bs, N, Fin), dtype=jnp.float32)
        adj = jax.random.randint(k2, (N, N), 0, 2, dtype=jnp.int32)
        W = jax.random.normal(k3, (Fin, Fout), dtype=jnp.float32) * (1.414 / np.sqrt(Fin))
        a = jax.random.normal(k4, (2 * Fout, 1), dtype=jnp.float32) * 0.1
        return {'x': x, 'adj': adj, 'W': W, 'a': a}
    _L0_gnn_all = _L0_gnn_setup()
    _L0_gnn_in = {k: v for k, v in _L0_gnn_all.items() if k in ('W', 'a', )}
    del _L0_gnn_all

    def _L1_gnn_setup():
        import jax, jax.numpy as jnp
        import numpy as np
        EPS = 1e-05

        def _layernorm(x, g, b):
            mu = jnp.mean(x, axis=-1, keepdims=True)
            var = jnp.mean(jnp.square(x - mu), axis=-1, keepdims=True)
            return (x - mu) * jax.lax.rsqrt(var + EPS) * g + b
        key = jax.random.key(seed)
        ks = jax.random.split(key, 8)
        F, N, C, H = (4096, 64, 256, 8)
        x = jax.random.normal(ks[0], (F, N, C), dtype=jnp.float32)
        adj = jax.random.randint(ks[1], (N, N), 0, 2, dtype=jnp.int32)
        adj = jnp.maximum(adj, jnp.eye(N, dtype=jnp.int32))
        s = 1.0 / np.sqrt(C)
        w_qkv = jax.random.normal(ks[2], (C, 3 * C), dtype=jnp.float32) * s
        w1 = jax.random.normal(ks[3], (C, C), dtype=jnp.float32) * s
        b1 = jnp.zeros((C,), dtype=jnp.float32)
        w2 = jax.random.normal(ks[4], (C, C), dtype=jnp.float32) * s
        b2 = jnp.zeros((C,), dtype=jnp.float32)
        ln1_g = jnp.ones((C,), jnp.float32)
        ln1_b = jnp.zeros((C,), jnp.float32)
        ln2_g = jnp.ones((C,), jnp.float32)
        ln2_b = jnp.zeros((C,), jnp.float32)
        return {'x': x, 'adj': adj, 'w_qkv': w_qkv, 'ln1_g': ln1_g, 'ln1_b': ln1_b, 'ln2_g': ln2_g, 'ln2_b': ln2_b, 'w1': w1, 'b1': b1, 'w2': w2, 'b2': b2}
    _L1_gnn_all = _L1_gnn_setup()
    _L1_gnn_in = {k: v for k, v in _L1_gnn_all.items() if k in ('w_qkv', 'ln1_g', 'ln1_b', 'ln2_g', 'ln2_b', 'w1', 'b1', 'w2', 'b2', )}
    del _L1_gnn_all

    def _L2_gnn_setup():
        import jax, jax.numpy as jnp
        import numpy as np
        IN_DIM = 256
        OUT_DIM = 64
        NUM_HEADS = 4
        ALPHA = 0.2
        NEG_INF = -9000000000000000.0
        key = jax.random.key(seed)
        k1, k2, k3, k4 = jax.random.split(key, 4)
        B, N = (4, 2048)
        h = jax.random.normal(k1, (B, N, IN_DIM), dtype=jnp.float32)
        adj = jax.random.randint(k2, (N, N), 0, 2, dtype=jnp.int32)
        W = jax.random.normal(k3, (IN_DIM, NUM_HEADS * OUT_DIM), dtype=jnp.float32) * (1.0 / np.sqrt(IN_DIM))
        a = jax.random.normal(k4, (2 * OUT_DIM,), dtype=jnp.float32) * (1.0 / np.sqrt(2 * OUT_DIM))
        return {'h': h, 'adj': adj, 'W': W, 'a': a}
    _L2_gnn_all = _L2_gnn_setup()
    _L2_gnn_in = {k: v for k, v in _L2_gnn_all.items() if k in ('W', 'a', )}
    del _L2_gnn_all

    def _L3_gnn_setup():
        import jax, jax.numpy as jnp
        import numpy as np
        ALPHA = 0.2
        NEG_INF = -1000000000000.0
        key = jax.random.key(seed)
        k1, k2, k3, k4, k5 = jax.random.split(key, 5)
        B, N, C_in, C_out = (8, 2048, 256, 256)
        inp = jax.random.normal(k1, (B, N, C_in), dtype=jnp.float32)
        adj = jax.random.randint(k2, (N, N), 0, 2, dtype=jnp.int32)
        limit = 1.414 * np.sqrt(6.0 / (C_in + C_out))
        W1 = jax.random.uniform(k3, (C_in, C_out), jnp.float32, -limit, limit)
        W2 = jax.random.uniform(k4, (C_in, C_out), jnp.float32, -limit, limit)
        W3 = jax.random.uniform(k5, (C_in, C_out), jnp.float32, -limit, limit)
        return {'inp': inp, 'adj': adj, 'W1': W1, 'W2': W2, 'W3': W3}
    _L3_gnn_all = _L3_gnn_setup()
    _L3_gnn_in = {k: v for k, v in _L3_gnn_all.items() if k in ('W1', 'W2', 'W3', )}
    del _L3_gnn_all

    return {
        "x": x,
        "adj": adj,
        "L0_gnn_W": _L0_gnn_in["W"],
        "L0_gnn_a": _L0_gnn_in["a"],
        "L1_gnn_w_qkv": _L1_gnn_in["w_qkv"],
        "L1_gnn_ln1_g": _L1_gnn_in["ln1_g"],
        "L1_gnn_ln1_b": _L1_gnn_in["ln1_b"],
        "L1_gnn_ln2_g": _L1_gnn_in["ln2_g"],
        "L1_gnn_ln2_b": _L1_gnn_in["ln2_b"],
        "L1_gnn_w1": _L1_gnn_in["w1"],
        "L1_gnn_b1": _L1_gnn_in["b1"],
        "L1_gnn_w2": _L1_gnn_in["w2"],
        "L1_gnn_b2": _L1_gnn_in["b2"],
        "L2_gnn_W": _L2_gnn_in["W"],
        "L2_gnn_a": _L2_gnn_in["a"],
        "L3_gnn_W1": _L3_gnn_in["W1"],
        "L3_gnn_W2": _L3_gnn_in["W2"],
        "L3_gnn_W3": _L3_gnn_in["W3"],
    }

def reference(x, adj, L0_gnn_W, L0_gnn_a, L1_gnn_w_qkv, L1_gnn_ln1_g, L1_gnn_ln1_b, L1_gnn_ln2_g, L1_gnn_ln2_b, L1_gnn_w1, L1_gnn_b1, L1_gnn_w2, L1_gnn_b2, L2_gnn_W, L2_gnn_a, L3_gnn_W1, L3_gnn_W2, L3_gnn_W3):
    import jax
    import jax.numpy as jnp
    def _L0_gnn_ref(x, adj, W, a):
        import jax, jax.numpy as jnp
        import numpy as np
        NEG_BIG = -9000000000000000.0
        alpha = 0.2
        h = jnp.matmul(x, W)
        Fout = h.shape[-1]
        a1, a2 = (a[:Fout, 0], a[Fout:, 0])
        s1 = jnp.einsum('bnf,f->bn', h, a1)
        s2 = jnp.einsum('bnf,f->bn', h, a2)
        e = jax.nn.leaky_relu(s1[:, :, None] + s2[:, None, :], negative_slope=alpha)
        attention = jnp.where(adj[None, :, :] > 0, e, NEG_BIG)
        attention = jax.nn.softmax(attention, axis=-1)
        h_prime = jnp.matmul(attention, h)
        return jax.nn.elu(h_prime)

    def _L1_gnn_ref(x, adj, w_qkv, ln1_g, ln1_b, ln2_g, ln2_b, w1, b1, w2, b2):
        import jax, jax.numpy as jnp
        import numpy as np
        EPS = 1e-05

        def _layernorm(x, g, b):
            mu = jnp.mean(x, axis=-1, keepdims=True)
            var = jnp.mean(jnp.square(x - mu), axis=-1, keepdims=True)
            return (x - mu) * jax.lax.rsqrt(var + EPS) * g + b
        F, N, C = x.shape
        H = 8
        D = C // H
        qkv = jnp.einsum('fnc,ck->fnk', x, w_qkv)
        q, k, v = jnp.split(qkv, 3, axis=-1)
        q = q.reshape(F, N, H, D)
        k = k.reshape(F, N, H, D)
        v = v.reshape(F, N, H, D)
        scores = jnp.einsum('fnhd,fmhd->fhnm', q, k) / jnp.sqrt(jnp.asarray(D, x.dtype))
        mask = (adj > 0)[None, None, :, :]
        scores = jnp.where(mask, scores, jnp.asarray(-1000000000.0, x.dtype))
        attn = jax.nn.softmax(scores, axis=-1)
        t = jnp.einsum('fhnm,fmhd->fnhd', attn, v).reshape(F, N, C)
        x = _layernorm(x + t, ln1_g, ln1_b)
        h = jax.nn.relu(jnp.einsum('fnc,cd->fnd', x, w1) + b1)
        f_out = jnp.einsum('fnd,dc->fnc', h, w2) + b2
        x = _layernorm(x + f_out, ln2_g, ln2_b)
        return x

    def _L2_gnn_ref(h, adj, W, a):
        import jax, jax.numpy as jnp
        import numpy as np
        IN_DIM = 256
        OUT_DIM = 64
        NUM_HEADS = 4
        ALPHA = 0.2
        NEG_INF = -9000000000000000.0
        B, N, _ = h.shape
        H, D = (NUM_HEADS, OUT_DIM)
        q = (h @ W).reshape(B, N, H, D)
        a_src, a_dst = (a[:D], a[D:])
        e_src = jnp.einsum('bnhd,d->bnh', q, a_src)
        e_dst = jnp.einsum('bnhd,d->bnh', q, a_dst)
        e = e_src[:, :, None, :] + e_dst[:, None, :, :]
        e = jnp.where(e >= 0, e, ALPHA * e)
        mask = (adj > 0)[None, :, :, None]
        e = jnp.where(mask, e, NEG_INF)
        attn = jax.nn.softmax(e, axis=2)
        h_prime = jnp.einsum('bijh,bjhd->bihd', attn, q)
        return jax.nn.elu(h_prime.reshape(B, N, H * D))

    def _L3_gnn_ref(inp, adj, W1, W2, W3):
        import jax, jax.numpy as jnp
        import numpy as np
        ALPHA = 0.2
        NEG_INF = -1000000000000.0
        h1 = jnp.einsum('bnc,cd->bnd', inp, W1)
        h2 = jnp.einsum('bnc,cd->bnd', inp, W2)
        h3 = jnp.einsum('bnc,cd->bnd', inp, W3)
        e = jnp.einsum('bnd,bmd->bnm', h1, h2)
        e = jax.nn.leaky_relu(e, ALPHA)
        e = jnp.where(adj[None, :, :] > 0, e, NEG_INF)
        attention = jax.nn.softmax(e, axis=-1)
        h_prime = jnp.einsum('bnm,bmd->bnd', attention, h3)
        return jax.nn.relu(h_prime)

    x = _layernorm(x + _L0_gnn_ref(x, adj, L0_gnn_W, L0_gnn_a), axis=-1)
    x = _layernorm(x + _L1_gnn_ref(x, adj, L1_gnn_w_qkv, L1_gnn_ln1_g, L1_gnn_ln1_b, L1_gnn_ln2_g, L1_gnn_ln2_b, L1_gnn_w1, L1_gnn_b1, L1_gnn_w2, L1_gnn_b2), axis=-1)
    x = _layernorm(x + _L2_gnn_ref(x, adj, L2_gnn_W, L2_gnn_a), axis=-1)
    x = _layernorm(x + _L3_gnn_ref(x, adj, L3_gnn_W1, L3_gnn_W2, L3_gnn_W3), axis=-1)
    return x


_drawn_inputs = setup_inputs


def setup_inputs(seed=0):
    import zlib

    import numpy as np

    out = dict(_drawn_inputs(seed))
    spreads = {'L1_gnn_ln1_g': (1.0, 0.2),
     'L1_gnn_ln1_b': (0.0, 0.1),
     'L1_gnn_ln2_g': (1.0, 0.2),
     'L1_gnn_ln2_b': (0.0, 0.1),
     'L1_gnn_b1': (0.0, 0.1),
     'L1_gnn_b2': (0.0, 0.1)}
    factors = {}
    for name, (base, spread) in spreads.items():
        noise = np.random.default_rng([zlib.crc32(name.encode()), seed]).standard_normal(out[name].shape)
        drawn = base * np.exp(spread * noise) if base else spread * noise
        out[name] = jnp.asarray(drawn.astype(out[name].dtype))
    for name, factor in factors.items():
        out[name] = (out[name] * factor).astype(out[name].dtype)
    return out
```

```python
import concourse.bass as bass
from concourse import mybir
from contextlib import ExitStack


def graph_layers_kernel(
    nc: bass.Bass,
    x: bass.AP,
    adj: bass.AP,
    gat_w: bass.AP,
    gat_a: bass.AP,
    w_qkv: bass.AP,
    ln1_g: bass.AP,
    ln1_b: bass.AP,
    ln2_g: bass.AP,
    ln2_b: bass.AP,
    ffn_w1: bass.AP,
    ffn_b1: bass.AP,
    ffn_w2: bass.AP,
    ffn_b2: bass.AP,
    mh_w: bass.AP,
    mh_a: bass.AP,
    dot_w1: bass.AP,
    dot_w2: bass.AP,
    dot_w3: bass.AP,
    out: bass.AP,
):
    f32 = mybir.dt.float32
    f16 = mybir.dt.float16
    bf16 = mybir.dt.bfloat16
    i32 = mybir.dt.int32
    ALU = mybir.AluOpType
    ACT = mybir.ActivationFunctionType

    P = 128
    B, N, C = x.shape
    NB = N // P
    CT = C // P
    SLOTS = 2
    TURNS = B // SLOTS
    WSCALE = 64.0
    SLOPE = 0.2
    EPS = 1e-5
    MASKED = 1e30
    BIG = 3e38
    QK_SCALE = 32.0 ** -0.5
    RSQRT_SEED = float(0x5F3759DF)
    HEADS = [1, 8, 4, 1]
    LAYERS = len(HEADS)
    LEAKY = [True, False, True, True]
    D1 = C // HEADS[1]
    COPIES = P // D1

    UNITS = [h * NB for h in HEADS]
    UNIT0 = [SLOTS * sum(UNITS[:l]) for l in range(LAYERS)]
    UNIT_TURN = SLOTS * sum(UNITS)
    LEAKY0 = [SLOTS * sum(UNITS[m] for m in range(l) if LEAKY[m]) for l in range(LAYERS)]
    LEAKY_TURN = SLOTS * sum(UNITS[m] for m in range(LAYERS) if LEAKY[m])
    RING = 4
    LAG_HI = 1
    LAG_T = 3
    LAG_PV = 4
    ACT_EVAC = (1, 3)
    DVE_EVAC = tuple(b for b in range(NB) if b not in ACT_EVAC)

    GROUPS = [
        [("xt", 0), ("xt", 1), ("h0", 0), ("h0", 1), ("s0", 0)],
        [("xt", 0), ("xt", 1), ("q", 0), ("q", 1), ("k", 0), ("k", 1), ("v", 0), ("v", 1)],
        [("xt", 0), ("xt", 1), ("f1", 0), ("f1", 1), ("f2", 0), ("f2", 1)],
        [("xt", 0), ("xt", 1), ("h2", 0), ("h2", 1), ("s2", 0)],
        [("xt", 0), ("xt", 1), ("g", 0), ("g", 1), ("h3", 0), ("h3", 1)],
    ]
    GROUP_OF = [0, 1, 3, 4]
    FFN = 2
    JOB0 = [sum(len(g) for g in GROUPS[:n]) for n in range(len(GROUPS) + 1)]
    JOB_TURN = SLOTS * JOB0[-1]

    def job_end(group, j, slot):
        return SLOTS * (JOB0[group] + j) + slot + 1

    ctx = ExitStack()
    with ctx:
        def sb(name, shape, dt=f32):
            return ctx.enter_context(nc.sbuf_tensor(name, shape, dt))

        def pb(name, shape, dt=f32):
            return ctx.enter_context(nc.psum_tensor(name, shape, dt))

        def sem(name):
            return ctx.enter_context(nc.semaphore(name))

        ident32 = sb("ident32", [P, P])
        ident16 = sb("ident16", [P, P], f16)
        identb = sb("identb", [P, P], bf16)
        neg_mask = sb("neg_mask", [P, NB, N], bf16)
        sel_row = sb("sel_row", [P, HEADS[2], N], f16)
        sel_col = sb("sel_col", [P, HEADS[2], P], f16)
        W = {k: sb(f"w_{k}", [P, 2, CT, C], f16) for k in ("h0", "q", "k", "v", "f1", "f2", "h2", "g", "h3")}
        W["s0"] = sb("w_s0", [P, 2, CT, P], f16)
        W["s2"] = sb("w_s2", [P, 2, CT, P], f16)
        rows = {k: sb(f"row_{k}", [P, C]) for k in ("g1", "b1", "g2", "b2", "fb2")}
        ffn_bias = sb("ffn_bias", [P, CT])

        S2 = range(SLOTS)
        xin = [sb(f"xin{s}", [P, NB, C]) for s in S2]
        xcur = [sb(f"xcur{s}", [P, NB, C]) for s in S2]
        xout = [sb(f"xout{s}", [P, NB, C]) for s in S2]
        za = [sb(f"za{s}", [P, NB, C]) for s in S2]
        zb = [sb(f"zb{s}", [P, NB, C]) for s in S2]
        xt = [sb(f"xt{s}", [P, 2, CT, N], f16) for s in S2]
        qk = [sb(f"qk{s}", [P, 2, 2, CT, N], f16) for s in S2]
        proj = [qk[s][:, :, 0] for s in S2]
        proj_k = [qk[s][:, :, 1] for s in S2]
        val = [sb(f"val{s}", [P, 2, NB, C], f16) for s in S2]
        s12 = [sb(f"s12_{s}", [P, N], f16) for s in S2]
        qk4 = [sb(f"qk4_{s}", [P, 2, CT, P // D1, N], f16) for s in S2]
        rowsum = [sb(f"rowsum{s}", [P, NB, HEADS[1]]) for s in S2]
        rinv = [sb(f"rinv{s}", [P, NB, HEADS[1]]) for s in S2]
        stats = [sb(f"stats{s}", [P, NB, 6]) for s in S2]
        small = [sb(f"small{s}", [P, 8, NB]) for s in S2]

        relu_r = sb("relu_r", [P, RING, N])
        masked_r = sb("masked_r", [P, RING, N])
        low_r = sb("low_r", [P, RING])
        prob_r = sb("prob_r", [P, RING, N])
        split_r = sb("split_r", [P, RING, 2, N], f16)
        trans_r = sb("trans_r", [P, RING, 2, NB, P], f16)

        scores_ps = [pb(f"scores_ps{i}", [P, N]) for i in range(2)]
        trans_ps = [pb(f"trans_ps{i}", [P, 2, NB, P], f16) for i in range(2)]
        acc_ps = [pb(f"acc_ps{s}", [P, NB, C]) for s in S2]

        CREDIT = 8

        def counted(name, per_turn):
            return sem(name), per_turn

        scores_done = counted("scores_done", UNIT_TURN)
        trans_done = counted("trans_done", UNIT_TURN)
        slot_done = [counted(f"slot_done{s}", LAYERS) for s in S2]
        dense_full = counted("dense_full", JOB_TURN)
        relu_done = counted("relu_done", LEAKY_TURN)
        probs_done = counted("probs_done", UNIT_TURN)
        evac_act = counted("evac_act", UNIT_TURN // NB * len(ACT_EVAC))
        dense_hi = counted("dense_hi", JOB_TURN)
        elu_exp = [counted(f"elu_exp{s}", 2) for s in S2]
        masked_done = counted("masked_done", UNIT_TURN)
        hi_done = counted("hi_done", UNIT_TURN)
        evac_dve = counted("evac_dve", UNIT_TURN // NB * len(DVE_EVAC))
        dense_lo = counted("dense_lo", JOB_TURN)
        elu_min = [counted(f"elu_min{s}", 2) for s in S2]
        x_ready = [counted(f"x_ready{s}", 4) for s in S2]
        out_ready = [counted(f"out_ready{s}", 1) for s in S2]
        lo_done = counted("lo_done", UNIT_TURN)
        x_loaded = [sem(f"x_loaded{s}") for s in S2]
        stacked = [sem(f"stacked{s}") for s in S2]
        out_stored = [sem(f"out_stored{s}") for s in S2]
        OUT_CREDIT = 16
        Q_PART = [c // 2 for c in range(COPIES)]
        K_PART = [c % 2 for c in range(COPIES)]
        STACKS = [(slice(0, 2), c, Q_PART[c]) for c in range(COPIES) if Q_PART[c] == K_PART[c]]
        STACKS += [(slice(w, w + 1), c, (Q_PART, K_PART)[w][c]) for c in range(COPIES) if Q_PART[c] != K_PART[c] for w in range(2)]
        STACK_DMAS = len(STACKS) * (P // D1)

        NORM_LINKS = 2 * NB + 17
        CHAIN_TURN = SLOTS * (2 * (NORM_LINKS + 3)
                              + NORM_LINKS + 2
                              + NORM_LINKS + 5
                              + CT
                              + 2 * NORM_LINKS + 2)
        dve_chain = counted("dve_chain", CHAIN_TURN)

        w_loaded = sem("w_loaded")
        ident_ready = sem("ident_ready")
        setup_pool = sem("setup_pool")
        setup_dve = sem("setup_dve")
        setup_pe = sem("setup_pe")
        dve_setup_chain = sem("dve_setup_chain")
        masking = sem("masking")
        credit_cell = sb("credit_cell", [P, 4])

        stage_w = {k: buf[0][:, CT * half:CT * half + CT, :]
                   for buf, keys in ((xcur, ("h0", "q")), (xout, ("k", "v")), (za, ("f1", "f2")), (zb, ("h2", "h3")))
                   for half, k in enumerate(keys)}
        stage_d1 = zb[1][:, 0:CT, :]
        stage_d2 = zb[1][:, CT:2 * CT, :]
        stage_t1 = za[1][:, 0:CT, :]
        stage_t2 = za[1][:, CT:2 * CT, :]
        stage_g = xcur[1][:, 0:CT, :]
        stage_s0 = xcur[1][:, CT, :].rearrange("p (t n) -> p t n", t=CT)
        stage_s2 = xcur[1][:, CT + 1, :].rearrange("p (t n) -> p t n", t=CT)
        stage_a0 = xout[1][:, 0:2, :]
        stage_a2 = xout[1][:, 2, 0:C // 2]
        stage_scratch = xout[1][:, 3, :]
        stage_adj = masked_r[:, :, :].bitcast(i32)
        stage_flag = prob_r

        block = ctx.enter_context(nc.Block())

        def at(it, counter, n):
            return it * counter[1] + (n + CREDIT)

        def wait(eng, it, counter, n):
            eng.wait_ge(counter[0], at(it, counter, n))

        def w_view(w):
            return w.rearrange("(t p) n -> p t n", p=P)

        def units(layer):
            return [(s * UNITS[layer] + h * NB + b, s, h, b)
                    for s in S2 for h in range(HEADS[layer]) for b in range(NB)]

        def evac_index(layer, k, b, which):
            return (UNIT0[layer] + k) // NB * len(which) + which.index(b) + 1

        @block.sync
        def _(sp):
            for k, src in (("h0", gat_w), ("q", w_qkv[:, 0:C]), ("k", w_qkv[:, C:2 * C]), ("v", w_qkv[:, 2 * C:3 * C]),
                           ("f1", ffn_w1), ("f2", ffn_w2), ("h2", mh_w), ("h3", dot_w3)):
                sp.dma_start(stage_w[k], w_view(src)).then_inc(w_loaded, 16)
            sp.dma_start(stage_d1, w_view(dot_w1)).then_inc(w_loaded, 16)
            sp.dma_start(stage_d2, w_view(dot_w2)).then_inc(w_loaded, 16)
            for k, src in (("g1", ln1_g), ("b1", ln1_b), ("g2", ln2_g), ("b2", ln2_b), ("fb2", ffn_b2)):
                sp.dma_start(rows[k][:], src.rearrange("(o n) -> o n", o=1).broadcast_to([P, C])).then_inc(w_loaded, 16)
            sp.dma_start(ffn_bias[:], ffn_b1.rearrange("(t p) -> p t", p=P), allow_slow_non_contiguous=True).then_inc(w_loaded, 16)
            sp.dma_start(stage_a0, gat_a.rearrange("(t n) o -> o t n", t=2).broadcast_to([P, 2, C])).then_inc(w_loaded, 16)
            sp.dma_start(stage_a2, mh_a.rearrange("(o n) -> o n", o=1).broadcast_to([P, C // 2])).then_inc(w_loaded, 16)
            sp.dma_start(stage_adj, adj.rearrange("(b p) n -> p b n", p=P)).then_inc(w_loaded, 16)

            def load_x(turn, s):
                sp.dma_start(xin[s][:], x[turn * SLOTS + s].rearrange("(b p) c -> p b c", p=P)).then_inc(x_loaded[s], 16)

            for s in S2:
                load_x(0, s)

            def turn(it, last):
                for s in S2:
                    if not last:
                        wait(sp, it, x_ready[s], 1)
                        load_x(it + 1, s)
                for s in S2:
                    g = GROUP_OF[1]
                    wait(sp, it, dense_lo, job_end(g, GROUPS[g].index(("k", CT - 1)), s))
                    for h in range(P // D1):
                        for which, c, part in STACKS:
                            sp.dma_start(qk4[s][c * D1:(c + 1) * D1, which, :, h, :],
                                         qk[s][h * D1:(h + 1) * D1, part, which, :, :]).then_inc(stacked[s], 16)
                for s in S2:
                    wait(sp, it, out_ready[s], 1)
                    sp.dma_start(out[it * SLOTS + s].rearrange("(b p) c -> p b c", p=P), xout[s][:]).then_inc(out_stored[s], 16)

            if TURNS > 1:
                with sp.Fori(0, TURNS - 1) as it:
                    turn(it, False)
            turn(TURNS - 1, True)
            for s in S2:
                sp.wait_ge(out_stored[s], 16 * TURNS + OUT_CREDIT)

        @block.gpsimd
        def _(pool):
            nc.gpsimd.memset(ident32[:], 0.0).then_inc(setup_pool, 1)
            nc.gpsimd.memset(sel_row[:], 0.0).then_inc(setup_pool, 1)
            nc.gpsimd.memset(sel_col[:], 0.0).then_inc(setup_pool, 1)
            pool.wait_ge(setup_pool, 3)
            nc.gpsimd.affine_select(out=ident32[:], in_=ident32[:], compare_op=ALU.not_equal, fill=1.0, base=0,
                                    pattern=[[-1, P]], channel_multiplier=1).then_inc(ident_ready, 1)
            for n, (tile, at_row) in enumerate(((sel_row, 0), (sel_row, 32), (sel_col, 64), (sel_col, 96))):
                width = tile.shape[2]
                nc.gpsimd.affine_select(out=tile[:], in_=tile[:], compare_op=ALU.not_equal, fill=1.0,
                                        base=-at_row, pattern=[[-1, HEADS[2]], [0, width]],
                                        channel_multiplier=1).then_inc(setup_pool, 1)
                pool.wait_ge(setup_pool, 4 + n)
            nc.gpsimd.memset(credit_cell[:, 0:1], 0.0).then_inc(lo_done[0], CREDIT)
            for s in S2:
                nc.gpsimd.memset(credit_cell[:, 1 + s:2 + s], 0.0).then_inc(out_stored[s], OUT_CREDIT)

            with pool.Fori(0, TURNS) as it:
                for layer in range(LAYERS):
                    for k, s, h, b in units(layer):
                        u = UNIT0[layer] + k
                        wait(pool, it, hi_done, u + 1)
                        wait(pool, it, trans_done, u + 1 - RING)
                        nc.gpsimd.tensor_tensor(split_r[:, u % RING, 1, :], prob_r[:, u % RING, :],
                                                split_r[:, u % RING, 0, :], ALU.subtract).then_inc(lo_done[0], 1)

        @block.scalar
        def _(act):
            credit_act = [relu_done, probs_done, evac_act, dense_hi, *elu_exp]
            act.wait_ge(ident_ready, 1)
            for n, counter in enumerate(credit_act):
                nc.scalar.copy(small[1][0:1, n, 0:1], ident32[0:1, 0:1]).then_inc(counter[0], CREDIT)

            def dense(it, group):
                for j, (kind, n) in enumerate(GROUPS[group]):
                    for s in S2:
                        bank = acc_ps[s][:, 2 * (j % 2):2 * (j % 2) + 2, :].rearrange("p a c -> p (a c)")
                        wait(act, it, dense_full, job_end(group, j, s))
                        if kind == "xt":
                            ins = nc.scalar.copy(xt[s][:, 0, n, :], bank)
                        elif kind in ("q", "k", "g"):
                            dst = proj_k if kind == "k" else proj
                            scale = {"q": QK_SCALE, "k": 1.0, "g": SLOPE}[kind] / WSCALE
                            ins = nc.scalar.activation(dst[s][:, 0, n, :], bank, ACT.Copy, scale=scale)
                        elif kind in ("s0", "s2"):
                            ins = nc.scalar.activation(s12[s][:], bank, ACT.Copy, scale=1.0 / WSCALE)
                        elif kind == "f1":
                            ins = nc.scalar.activation(za[s][:, 2 * n:2 * n + 2, :].rearrange("p a c -> p (a c)"), bank,
                                                       ACT.Relu, bias=ffn_bias[:, n:n + 1], scale=1.0 / WSCALE)
                        elif kind == "f2":
                            ins = nc.scalar.activation(za[s][:, 2 * n:2 * n + 2, :].rearrange("p a c -> p (a c)"), bank,
                                                       ACT.Copy, scale=1.0 / WSCALE)
                        else:
                            ins = nc.scalar.activation(val[s][:, 0, 2 * n:2 * n + 2, :].rearrange("p a c -> p (a c)"), bank,
                                                       ACT.Copy, scale=1.0 / WSCALE)
                        ins.then_inc(dense_hi[0], 1)

            def attention(it, layer):
                todo = units(layer)

                def relu(k):
                    u = UNIT0[layer] + k
                    wait(act, it, scores_done, u + 1)
                    wait(act, it, masked_done, u + 1 - RING)
                    nc.scalar.activation(relu_r[:, u % RING, :], scores_ps[u % 2][:], ACT.Relu,
                                         scale=1.0 / SLOPE - 1.0).then_inc(relu_done[0], 1)

                def probs(k):
                    u = UNIT0[layer] + k
                    _, s, h, b = todo[k]
                    wait(act, it, masked_done, u + 1)
                    wait(act, it, lo_done, u + 1 - RING)
                    nc.scalar.activation(prob_r[:, u % RING, :], masked_r[:, u % RING, :], ACT.Exp,
                                         bias=low_r[:, u % RING:u % RING + 1], scale=-1.0,
                                         accum_out=rowsum[s][:, b, h:h + 1]).then_inc(probs_done[0], 1)

                def evac(k):
                    u = UNIT0[layer] + k
                    b = todo[k][3]
                    if b in ACT_EVAC:
                        wait(act, it, trans_done, u + 1)
                        nc.scalar.copy(trans_r[:, u % RING], trans_ps[u % 2][:]).then_inc(evac_act[0], 1)

                for step in range(len(todo) + LAG_T):
                    if LEAKY[layer] and step < len(todo):
                        relu(step)
                    if 0 <= step - LAG_T:
                        evac(step - LAG_T)
                    if step < len(todo):
                        probs(step)

            def elu(it, n, s):
                wait(act, it, elu_min[s], n + 1)
                nc.scalar.activation(zb[s][:], zb[s][:], ACT.Exp).then_inc(elu_exp[s][0], 1)

            with act.Fori(0, TURNS) as it:
                for layer in range(LAYERS):
                    dense(it, GROUP_OF[layer])
                    attention(it, layer)
                    if layer in (0, 2):
                        for s in S2:
                            elu(it, layer // 2, s)
                    if layer == 1:
                        dense(it, FFN)

        @block.vector
        def _(dve):
            setup = [0]

            def after(ins):
                setup[0] += 1
                ins.then_inc(dve_setup_chain, 1)
                dve.wait_ge(dve_setup_chain, setup[0])

            for n, counter in enumerate([masked_done, hi_done, evac_dve, dense_lo, *elu_min, *x_ready, *out_ready, dve_chain]):
                nc.vector.memset(stats[0][:, n % NB, n // NB:n // NB + 1], 0.0).then_inc(counter[0], CREDIT)
            dve.wait_ge(w_loaded, 16 * 19)
            dve.wait_ge(ident_ready, 1)
            nc.vector.tensor_copy(ident16[:], ident32[:])
            after(nc.vector.tensor_copy(identb[:], ident32[:]))
            after(nc.vector.tensor_scalar(stage_flag[:], stage_adj, 0.0, 1.0, ALU.is_gt, ALU.subtract))
            after(nc.vector.tensor_scalar(neg_mask[:], stage_flag[:], MASKED, None, ALU.mult))

            def split_weight(dst, src, scale):
                after(nc.vector.tensor_scalar(dst[:, 0], src, scale, None, ALU.mult))
                after(nc.vector.scalar_tensor_tensor(out=dst[:, 1], in0=src, scalar=scale, in1=dst[:, 0],
                                                     op0=ALU.mult, op1=ALU.subtract))

            for key, stage_s, heads, stage_src in (("s0", stage_s0, 1, stage_w["h0"]), ("s2", stage_s2, HEADS[2], stage_w["h2"])):
                after(nc.vector.memset(stage_s, 0.0))
                width = C // heads
                for h in range(heads):
                    for side in range(2):
                        for t in range(CT):
                            a = stage_a0[:, side, :] if heads == 1 else stage_a2[:, side * width:(side + 1) * width]
                            col = 64 * side + h
                            after(nc.vector.tensor_tensor_reduce(
                                out=stage_scratch[:, 0:width], in0=stage_src[:, t, h * width:(h + 1) * width], in1=a,
                                scale=1.0, scalar=0.0, op0=ALU.mult, op1=ALU.add, accum_out=stage_s[:, t, col:col + 1]))
                for side in range(2):
                    after(nc.vector.tensor_copy(stage_s[:, :, 64 * side + 32:64 * side + 32 + heads],
                                                stage_s[:, :, 64 * side:64 * side + heads]))
                split_weight(W[key], stage_s, WSCALE * SLOPE)
            for k in ("h0", "q", "k", "v", "f1", "f2", "h2", "h3"):
                split_weight(W[k], stage_w[k], WSCALE)
            dve.wait_ge(setup_pe, 1)
            nc.vector.tensor_copy(stage_t1, acc_ps[0][:, 0:2, :])
            nc.vector.tensor_copy(stage_t2, acc_ps[0][:, 2:4, :]).then_inc(setup_dve, 1)
            dve.wait_ge(setup_pe, 2)
            after(nc.vector.tensor_copy(stage_g, acc_ps[1][:, 0:2, :]))
            split_weight(W["g"], stage_g, WSCALE)
            nc.vector.memset(credit_cell[:, 3:4], 0.0).then_inc(setup_dve, 1)

            chain = [0]

            def mark(ins):
                chain[0] += 1
                ins.then_inc(dve_chain[0], 1)
                return chain[0]

            def own(it, n):
                wait(dve, it, dve_chain, n)

            def dense(it, group):
                for j, (kind, n) in enumerate(GROUPS[group]):
                    for s in S2:
                        bank = acc_ps[s][:, 2 * (j % 2):2 * (j % 2) + 2, :].rearrange("p a c -> p (a c)")
                        wait(dve, it, dense_hi, job_end(group, j, s))

                        def lo(dst, hi, scale):
                            return nc.vector.scalar_tensor_tensor(out=dst, in0=bank, scalar=scale, in1=hi,
                                                                  op0=ALU.mult, op1=ALU.subtract)

                        if kind == "xt":
                            ins = lo(xt[s][:, 1, n, :], xt[s][:, 0, n, :], 1.0)
                        elif kind in ("q", "k", "g"):
                            dst = proj_k if kind == "k" else proj
                            scale = {"q": QK_SCALE, "k": 1.0, "g": SLOPE}[kind] / WSCALE
                            ins = lo(dst[s][:, 1, n, :], dst[s][:, 0, n, :], scale)
                        elif kind in ("s0", "s2"):
                            for q in (1, 3):
                                r = slice(32 * q, 32 * q + 32)
                                ins = nc.vector.scalar_tensor_tensor(out=s12[s][r, :], in0=bank[r, :], scalar=1.0 / WSCALE,
                                                                     in1=s12[s][r, :], op0=ALU.mult, op1=ALU.subtract)
                        elif kind == "f1":
                            hid = za[s][:, 2 * n:2 * n + 2, :].rearrange("p a c -> p (a c)")
                            own(it, mark(nc.vector.tensor_copy(proj[s][:, 0, n, :], hid)))
                            ins = nc.vector.tensor_tensor(proj[s][:, 1, n, :], hid, proj[s][:, 0, n, :], ALU.subtract)
                        elif kind == "f2":
                            ins = nc.vector.tensor_tensor(za[s][:, 2 * n:2 * n + 2, :], za[s][:, 2 * n:2 * n + 2, :],
                                                          zb[s][:, 2 * n:2 * n + 2, :], ALU.add)
                        else:
                            v = [val[s][:, p, 2 * n:2 * n + 2, :].rearrange("p a c -> p (a c)") for p in range(2)]
                            ins = lo(v[1], v[0], 1.0 / WSCALE)
                        ins.then_inc(dense_lo[0], 1)

            def normed(it, slots, src, dst, ready):
                last = {}
                for s in slots:
                    for b in range(NB):
                        last[s] = mark(nc.vector.bn_stats(stats[s][:, b, :], src[s][:, b, :]))

                def each(f):
                    for s in slots:
                        own(it, last[s])
                        last[s] = mark(f(s))

                def col(s, n):
                    return small[s][:, n, :]

                MEAN, DIFF, VAR, SQ, Y0, Y1, T0, T1 = range(8)
                each(lambda s: nc.vector.tensor_tensor(col(s, DIFF), stats[s][:, :, 1], stats[s][:, :, 4], ALU.subtract))
                each(lambda s: nc.vector.tensor_tensor(col(s, MEAN), stats[s][:, :, 1], stats[s][:, :, 4], ALU.add))
                each(lambda s: nc.vector.tensor_tensor(col(s, VAR), stats[s][:, :, 2], stats[s][:, :, 5], ALU.add))
                each(lambda s: nc.vector.tensor_scalar(col(s, MEAN), col(s, MEAN), 0.5, None, ALU.mult))
                each(lambda s: nc.vector.tensor_tensor(col(s, SQ), col(s, DIFF), col(s, DIFF), ALU.mult))
                each(lambda s: nc.vector.tensor_scalar(col(s, VAR), col(s, VAR), 1.0 / C, EPS, ALU.mult, ALU.add))
                each(lambda s: nc.vector.scalar_tensor_tensor(out=col(s, VAR), in0=col(s, SQ), scalar=0.25, in1=col(s, VAR),
                                                              op0=ALU.mult, op1=ALU.add))
                each(lambda s: nc.vector.tensor_scalar(col(s, Y0).bitcast(i32), col(s, VAR).bitcast(i32), -0.5, RSQRT_SEED,
                                                       ALU.mult, ALU.add))
                y, z = Y0, Y1
                for _ in range(3):
                    each(lambda s: nc.vector.scalar_tensor_tensor(out=col(s, T0), in0=col(s, y), scalar=-0.5, in1=col(s, y),
                                                                  op0=ALU.mult, op1=ALU.mult))
                    each(lambda s: nc.vector.tensor_tensor(col(s, T1), col(s, T0), col(s, VAR), ALU.mult))
                    each(lambda s: nc.vector.scalar_tensor_tensor(out=col(s, z), in0=col(s, T1), scalar=1.5, in1=col(s, y),
                                                                  op0=ALU.add, op1=ALU.mult))
                    y, z = z, y
                for s in slots:
                    own(it, last[s])
                    for b in range(NB):
                        ins = nc.vector.tensor_scalar(dst[s][:, b, :], src[s][:, b, :], small[s][:, MEAN, b:b + 1],
                                                      small[s][:, y, b:b + 1], ALU.subtract, ALU.mult)
                        if ready is None or b < NB - 1:
                            last[s] = mark(ins)
                        else:
                            ins.then_inc(ready[s][0], 1)
                            last[s] = None
                return last

            def divided(it, layer, slots):
                heads = HEADS[layer]
                last = {}
                for s in slots:
                    wait(dve, it, slot_done[s], layer + 1)
                    own(it, mark(nc.vector.reciprocal(rinv[s][:, :, 0:heads], rowsum[s][:, :, 0:heads])))
                    last[s] = mark(nc.vector.tensor_tensor(
                        za[s][:].rearrange("p b (h d) -> p b h d", h=heads),
                        acc_ps[s][:].rearrange("p b (h d) -> p b h d", h=heads),
                        rinv[s][:, :, 0:heads].unsqueeze(3).broadcast_to([P, NB, heads, C // heads]), ALU.mult))
                return last

            def finish(it, layer, slots):
                last = divided(it, layer, slots)
                old = xin if layer == 0 else xcur
                if layer in (0, 2):
                    for s in slots:
                        own(it, last[s])
                        nc.vector.tensor_scalar(zb[s][:], za[s][:], 0.0, None, ALU.min).then_inc(elu_min[s][0], 1)
                        last[s] = mark(nc.vector.scalar_tensor_tensor(out=za[s][:], in0=za[s][:], scalar=0.0, in1=old[s][:],
                                                                      op0=ALU.max, op1=ALU.add))
                    for s in slots:
                        own(it, last[s])
                        wait(dve, it, elu_exp[s], layer // 2 + 1)
                        last[s] = mark(nc.vector.scalar_tensor_tensor(out=za[s][:], in0=zb[s][:], scalar=-1.0, in1=za[s][:],
                                                                      op0=ALU.add, op1=ALU.add))
                    for s in slots:
                        own(it, last[s])
                    normed(it, slots, za, xcur, x_ready)
                elif layer == 3:
                    for s in slots:
                        own(it, last[s])
                        last[s] = mark(nc.vector.scalar_tensor_tensor(out=za[s][:], in0=za[s][:], scalar=0.0, in1=old[s][:],
                                                                      op0=ALU.max, op1=ALU.add))
                    for s in slots:
                        own(it, last[s])
                        dve.wait_ge(out_stored[s], it * 16 + OUT_CREDIT)
                    normed(it, slots, za, xout, out_ready)
                else:
                    for s in slots:
                        own(it, last[s])
                        last[s] = mark(nc.vector.tensor_tensor(za[s][:], za[s][:], xcur[s][:], ALU.add))
                    for s in slots:
                        own(it, last[s])
                    last = normed(it, slots, za, zb, None)
                    last = affine(it, slots, zb, zb, "g1", "b1", last, x1_ready=True)

            def affine(it, slots, src, dst, g, b, last, x1_ready=False):
                for s in slots:
                    own(it, last[s])
                    last[s] = mark(nc.vector.tensor_tensor(src[s][:], src[s][:], rows[g][:].unsqueeze(1).broadcast_to([P, NB, C]), ALU.mult))
                for s in slots:
                    own(it, last[s])
                    if x1_ready:
                        dve.wait_ge(out_stored[s], it * 16 + OUT_CREDIT)
                        ins = nc.vector.tensor_tensor(xout[s][:], src[s][:], rows[b][:].unsqueeze(1).broadcast_to([P, NB, C]), ALU.add)
                        n = mark(ins)
                        own(it, n)
                        nc.vector.tensor_tensor(zb[s][:], xout[s][:], rows["fb2"][:].unsqueeze(1).broadcast_to([P, NB, C]),
                                                ALU.add).then_inc(x_ready[s][0], 1)
                    else:
                        last[s] = mark(nc.vector.tensor_tensor(dst[s][:], src[s][:], rows[b][:].unsqueeze(1).broadcast_to([P, NB, C]), ALU.add))
                return last

            def finish_ffn(it):
                for s in S2:
                    wait(dve, it, dense_lo, job_end(FFN, len(GROUPS[FFN]) - 1, s))
                last = normed(it, S2, za, zb, None)
                last = affine(it, S2, zb, zb, "g2", "b2", last)
                for s in S2:
                    own(it, last[s])
                    last[s] = mark(nc.vector.tensor_tensor(za[s][:], zb[s][:], xcur[s][:], ALU.add))
                for s in S2:
                    own(it, last[s])
                normed(it, S2, za, xcur, x_ready)

            def attention(it, layer):
                todo = units(layer)

                def masked(k):
                    u = UNIT0[layer] + k
                    b = todo[k][3]
                    wait(dve, it, probs_done, u + 1 - RING)
                    if LEAKY[layer]:
                        wait(dve, it, relu_done, LEAKY0[layer] + k + 1)
                        second = relu_r[:, u % RING, :]
                    else:
                        wait(dve, it, scores_done, u + 1)
                        second = neg_mask[:, b, :]
                    dve.sem_inc(masking, 1)
                    nc.vector.tensor_tensor_reduce(out=masked_r[:, u % RING, :], in0=scores_ps[u % 2][:], in1=second,
                                                   scale=-1.0, scalar=BIG, op0=ALU.add, op1=ALU.min,
                                                   accum_out=low_r[:, u % RING:u % RING + 1]).then_inc(masked_done[0], 1)

                def hi(k):
                    u = UNIT0[layer] + k
                    wait(dve, it, probs_done, u + 1)
                    wait(dve, it, trans_done, u + 1 - RING)
                    nc.vector.tensor_copy(split_r[:, u % RING, 0, :], prob_r[:, u % RING, :]).then_inc(hi_done[0], 1)

                def evac(k):
                    u = UNIT0[layer] + k
                    if todo[k][3] in DVE_EVAC:
                        wait(dve, it, trans_done, u + 1)
                        nc.vector.tensor_copy(trans_r[:, u % RING], trans_ps[u % 2][:]).then_inc(evac_dve[0], 1)

                for step in range(len(todo) + LAG_T):
                    if step < len(todo):
                        masked(step)
                    if 0 <= step - LAG_T:
                        evac(step - LAG_T)
                    if 0 <= step - LAG_HI < len(todo):
                        hi(step - LAG_HI)

            with dve.Fori(0, TURNS) as it:
                for layer in range(LAYERS):
                    if layer == 0:
                        for s in S2:
                            dve.wait_ge(x_loaded[s], it * 16 + 16)
                    dense(it, GROUP_OF[layer])
                    attention(it, layer)
                    finish(it, layer, S2)
                    if layer == 1:
                        dense(it, FFN)
                        finish_ffn(it)
            assert chain[0] == CHAIN_TURN

        @block.tensor
        def _(pe):
            pe.wait_ge(ident_ready, 1)
            pe.wait_ge(w_loaded, 16 * 19)
            for half, src in enumerate((stage_d1, stage_d2)):
                for tf in range(CT):
                    for tc in range(CT):
                        ins = nc.tensor.transpose(acc_ps[0][:, 2 * half + tf, tc * P:(tc + 1) * P],
                                                  src[:, tc, tf * P:(tf + 1) * P], ident32[:])
            ins.then_inc(setup_pe, 1)
            pe.wait_ge(setup_dve, 1)
            for tc in range(CT):
                for tf in range(CT):
                    ins = nc.tensor.matmul(acc_ps[1][:, tc, :], stage_t1[:, tf, tc * P:(tc + 1) * P], stage_t2[:, tf, :],
                                           start=(tf == 0), stop=(tf == CT - 1))
            ins.then_inc(setup_pe, 1)
            for counter in [scores_done, trans_done, *slot_done, dense_full]:
                nc.tensor.transpose(scores_ps[0][:, 0:P], ident32[:], ident32[:]).then_inc(counter[0], CREDIT)
            pe.wait_ge(setup_dve, 2)
            pe.wait_ge(setup_pool, 7)

            TERMS = [(0, 0), (0, 1), (1, 0)]

            def dense(it, group):
                for j, (kind, n) in enumerate(GROUPS[group]):
                    for s in S2:
                        bank = acc_ps[s][:, 2 * (j % 2):2 * (j % 2) + 2, :]
                        flat = bank.rearrange("p a c -> p (a c)")
                        if j == 0:
                            if group == 0:
                                pe.wait_ge(x_loaded[s], it * 16 + 16)
                                wait(pe, it, out_ready[s], 0)
                            else:
                                wait(pe, it, x_ready[s], group)
                        if j >= 2:
                            wait(pe, it, dense_lo, job_end(group, j - 2, s))
                        if j == 2 or (kind == "f2" and n == 0):
                            wait(pe, it, dense_lo, job_end(group, j - 1, s))
                        if kind == "xt":
                            src = {0: xin, FFN: xout}.get(group, xcur)
                            for b in range(NB):
                                ins = nc.tensor.transpose(flat[:, b * P:(b + 1) * P], src[s][:, b, n * P:(n + 1) * P], ident32[:])
                        elif kind in ("q", "k", "g", "s0", "s2", "f1"):
                            i = 0
                            for t in range(CT):
                                for wp, xp in TERMS:
                                    ins = nc.tensor.matmul(flat, W[kind][:, wp, t, n * P:(n + 1) * P], xt[s][:, xp, t, :],
                                                           start=(i == 0), stop=(i == 3 * CT - 1))
                                    i += 1
                        else:
                            left = proj if kind == "f2" else xt
                            for half in range(2):
                                b = 2 * n + half
                                i = 0
                                for t in range(CT):
                                    for xp, wp in TERMS:
                                        ins = nc.tensor.matmul(bank[:, half, :], left[s][:, xp, t, b * P:(b + 1) * P],
                                                               W[kind][:, wp, t, :], start=(i == 0), stop=(i == 3 * CT - 1))
                                        i += 1
                        ins.then_inc(dense_full[0], 1)

            def attention(it, layer):
                todo = units(layer)
                heads = HEADS[layer]
                width = C // heads

                def scores(k):
                    u = UNIT0[layer] + k
                    _, s, h, b = todo[k]
                    ps = scores_ps[u % 2][:]
                    q = slice(b * P, (b + 1) * P)
                    if h == 0 and b == 0 and s == 0:
                        wait(pe, it, dense_lo, job_end(GROUP_OF[layer], len(GROUPS[GROUP_OF[layer]]) - 1, SLOTS - 1))
                    if layer == 1 and h == 0 and b == 0:
                        pe.wait_ge(stacked[s], it * (16 * STACK_DMAS) + 16 * STACK_DMAS)
                    wait(pe, it, masked_done, u - 1)
                    if layer == 1:
                        t, hq = divmod(h, P // D1)
                        ops = [(qk4[s][:, 0, t, hq, q], qk4[s][:, 1, t, hq, :])]
                    elif layer == 3:
                        ops = [(proj[s][:, gp, t, q], xt[s][:, xp, t, :]) for t in range(CT) for gp, xp in TERMS]
                    else:
                        ops = [(s12[s][:, q], sel_row[:, h, :]), (sel_col[:, h, :], s12[s][:])]
                    if layer != 1:
                        ops.append((identb[:], neg_mask[:, b, :]))
                    for i, (left, right) in enumerate(ops):
                        ins = nc.tensor.matmul(ps, left, right, start=(i == 0), stop=(i == len(ops) - 1))
                    ins.then_inc(scores_done[0], 1)

                def transposes(k):
                    u = UNIT0[layer] + k
                    wait(pe, it, lo_done, u + 1)
                    if k >= 2:
                        evacuated(k - 2)
                    for part in range(2):
                        for jb in range(NB):
                            ins = nc.tensor.transpose(trans_ps[u % 2][:, part, jb, :],
                                                      split_r[:, u % RING, part, jb * P:(jb + 1) * P], ident16[:])
                    ins.then_inc(trans_done[0], 1)

                def evacuated(k):
                    b = todo[k][3]
                    which, counter = (ACT_EVAC, evac_act) if b in ACT_EVAC else (DVE_EVAC, evac_dve)
                    wait(pe, it, counter, evac_index(layer, k, b, which))

                def values(k):
                    u = UNIT0[layer] + k
                    _, s, h, b = todo[k]
                    evacuated(k)
                    i = 0
                    for jb in range(NB):
                        for pp, vp in TERMS:
                            ins = nc.tensor.matmul(acc_ps[s][:, b, h * width:(h + 1) * width], trans_r[:, u % RING, pp, jb, :],
                                                   val[s][:, vp, jb, h * width:(h + 1) * width],
                                                   start=(i == 0), stop=(i == 3 * NB - 1))
                            i += 1
                    if h == heads - 1 and b == NB - 1:
                        ins.then_inc(slot_done[s][0], 1)

                for step in range(len(todo) + LAG_PV):
                    if step < len(todo):
                        scores(step)
                    if 0 <= step - LAG_T < len(todo):
                        transposes(step - LAG_T)
                    if 0 <= step - LAG_PV:
                        values(step - LAG_PV)

            with pe.Fori(0, TURNS) as it:
                for layer in range(LAYERS):
                    dense(it, GROUP_OF[layer])
                    attention(it, layer)
                    if layer == 1:
                        dense(it, FFN)


_INS = ['x', 'adj', 'L0_gnn_W', 'L0_gnn_a', 'L1_gnn_w_qkv', 'L1_gnn_ln1_g', 'L1_gnn_ln1_b', 'L1_gnn_ln2_g',
        'L1_gnn_ln2_b', 'L1_gnn_w1', 'L1_gnn_b1', 'L1_gnn_w2', 'L1_gnn_b2', 'L2_gnn_W', 'L2_gnn_a',
        'L3_gnn_W1', 'L3_gnn_W2', 'L3_gnn_W3']
_OUT = ((32, 512, 256), 'float32')


def kernel(**inputs):
    import numpy as _np
    import concourse.bacc as _bacc
    from concourse import mybir as _mybir
    from concourse.bass_utils import run_bass_kernel_spmd as _run

    nc = _bacc.Bacc("TRN2", target_bir_lowering=False, num_devices=1)
    arrays, args = {}, []
    for name in _INS:
        a = _np.ascontiguousarray(inputs[name])
        arrays[f"in_{name}_dram"] = a
        args.append(nc.dram_tensor(f"in_{name}_dram", a.shape, _mybir.dt.from_np(a.dtype), kind="ExternalInput").ap())
    shape, dtype = _OUT
    args.append(nc.dram_tensor("out_dram", shape, _mybir.dt.from_np(_np.dtype(dtype)), kind="ExternalOutput").ap())
    graph_layers_kernel(nc, *args)
    r = _run(nc, [arrays], core_ids=[0])
    return r.results[0]["out_dram"]
```

```python
import concourse.bass as bass
from concourse import mybir
from contextlib import ExitStack


def graph_layers_kernel(
    nc: bass.Bass,
    x: bass.AP,
    adj: bass.AP,
    gat_w: bass.AP,
    gat_a: bass.AP,
    w_qkv: bass.AP,
    ln1_g: bass.AP,
    ln1_b: bass.AP,
    ln2_g: bass.AP,
    ln2_b: bass.AP,
    ffn_w1: bass.AP,
    ffn_b1: bass.AP,
    ffn_w2: bass.AP,
    ffn_b2: bass.AP,
    mh_w: bass.AP,
    mh_a: bass.AP,
    dot_w1: bass.AP,
    dot_w2: bass.AP,
    dot_w3: bass.AP,
    out: bass.AP,
):
    f32 = mybir.dt.float32
    f16 = mybir.dt.float16
    bf16 = mybir.dt.bfloat16
    i32 = mybir.dt.int32
    ALU = mybir.AluOpType
    ACT = mybir.ActivationFunctionType

    P = 128
    B, N, C = x.shape
    NB = N // P
    CT = C // P
    SLOTS = 2
    TURNS = B // SLOTS
    WSCALE = 64.0
    SLOPE = 0.2
    EPS = 1e-5
    MASKED = 1e30
    BIG = 3e38
    QK_SCALE = 32.0 ** -0.5
    RSQRT_SEED = float(0x5F3759DF)
    HEADS = [1, 8, 4, 1]
    LAYERS = len(HEADS)
    LEAKY = [True, False, True, True]
    D1 = C // HEADS[1]
    COPIES = P // D1

    COST_UNIT = (1.65, 1.479, 1.9, 3.4)
    COST_JOB, COST_LINK, COST_FIN = (2.4, 0.3, 2.235)
    GAP_PIPE, GAP_JOBS, GAP_STACK = (6.0, 2.0, 14.0)
    OFFSET = 0.5
    RING = 4
    LAG_HI, LAG_T, LAG_PV = (1, 4, 5)
    LAG_P = 1
    ACT_EVAC = (1, 2, 3)
    DVE_EVAC = tuple(n for n in range(NB) if n not in ACT_EVAC)

    GROUPS = [
        [("xt", 0), ("xt", 1), ("h0", 0), ("h0", 1), ("s0", 0)],
        [("xt", 0), ("xt", 1), ("q", 0), ("q", 1), ("k", 0), ("k", 1), ("v", 0), ("v", 1)],
        [("xt", 0), ("xt", 1), ("f1", 0), ("f1", 1), ("f2", 0), ("f2", 1)],
        [("xt", 0), ("xt", 1), ("h2", 0), ("h2", 1), ("s2", 0)],
        [("xt", 0), ("xt", 1), ("g", 0), ("g", 1), ("h3", 0), ("h3", 1)],
    ]
    GROUP_OF = [0, 1, 3, 4]
    FFN = 2

    NORM = [("stats", b) for b in range(NB)] + [("aggregate",), ("add_eps",), ("seed",)] \
        + [("newton", n, part) for n in range(3) for part in range(3)]
    GAP = ("gap",)

    def norm(which):
        return [((*item, which), COST_LINK) for item in NORM]

    def applying(which):
        if which in (1, "ffn"):
            return [(("gain", which), 1.5 * COST_FIN), (("apply", which), 1.5 * COST_FIN)]
        return [(("apply", which), 1.0 * COST_FIN)]

    def finish(layer):
        work = [(GAP, GAP_PIPE), (("recip", layer), 0.5 * COST_FIN), (("divide", layer), 1.0 * COST_FIN)]
        if layer in (0, 2):
            work += [(("elu_min", layer), 2.0 * COST_FIN), (("elu_add", layer), 1.5 * COST_FIN)]
        else:
            work += [(("residual", layer), 1.5 * COST_FIN)]
        return work + norm(layer) + applying(layer)

    def group(g):
        return [(("job", g, j), COST_JOB) for j in range(len(GROUPS[g]))]

    def units(layer, cost):
        return [(("unit", layer, h, b), cost) for h in range(HEADS[layer]) for b in range(NB)]

    WORK = (group(0) + [(GAP, GAP_JOBS)] + units(0, COST_UNIT[0]) + finish(0) + [(("load",), 0.0)]
            + group(1)[:6] + [(("stack",), 0.0)] + group(1)[6:] + [(GAP, GAP_STACK)] + units(1, COST_UNIT[1]) + finish(1)
            + [(("affine", 1), 0.0)] + group(FFN) + [(GAP, GAP_JOBS)] + norm("ffn") + applying("ffn") + [(("affine", 2), 3.0)]
            + norm("out1") + applying("out1")
            + group(3) + [(GAP, GAP_JOBS)] + units(2, COST_UNIT[2]) + finish(2)
            + group(4) + [(GAP, GAP_JOBS)] + units(3, COST_UNIT[3]) + finish(3) + [(("store",), 0.0)])

    SPAN = sum(cost for _, cost in WORK)
    timed = []
    for s in range(SLOTS):
        t = 0.0
        for item, cost in WORK:
            when = t + s * SPAN * OFFSET
            if item != GAP:
                timed.append((when % SPAN, s, len(timed), item, when >= SPAN))
            t += cost
    timed.sort()
    ORDER = []
    pipe = []
    order_units = []
    for _, s, _, item, late in timed:
        if item[0] == "unit":
            order_units.append((item[1], s, item[2], item[3], late))
            pipe.append(len(order_units) - 1)
            ORDER.append((("step", len(pipe) - 1), s, late))
            continue
        if item[0] == "recip":
            last = max(n for n, u in enumerate(order_units) if u[0] == item[1] and u[1] == s)
            while len(pipe) - 1 < pipe.index(last) + LAG_PV:
                pipe.append(None)
                ORDER.append((("step", len(pipe) - 1), s, False))
        ORDER.append((item, s, late))
    while any(u is not None for u in pipe[-LAG_PV:]):
        pipe.append(None)
        ORDER.append((("step", len(pipe) - 1), 0, False))
    UNITS = order_units
    assert len(UNITS) % RING == 0 and len(UNITS) % NB == 0

    def counts(items):
        return {key: (place, n + 1, late) for n, (key, place, late) in enumerate(items)}

    def item_counts(kind, s):
        return counts((item[1:], place, late) for place, (item, slot, late) in enumerate(ORDER)
                      if item[0] == kind and slot == s)

    STEP_PLACE = {pipe[item[1]]: place for place, (item, _, _) in enumerate(ORDER)
                  if item[0] == "step" and pipe[item[1]] is not None}

    def unit_counts(s, of=lambda u: True):
        return counts((u, STEP_PLACE[u], UNITS[u][4]) for u in range(len(UNITS)) if UNITS[u][1] == s and of(u))

    LINKS = {"recip": 1, "divide": 1, "elu_min": 1, "elu_add": 1, "residual": 1, "stats": 1, "aggregate": 1,
             "add_eps": 1, "seed": 1, "newton": 1, "gain": 1}

    def links(item):
        if item[0] == "job":
            return 1 if GROUPS[item[1]][item[2]][0] == "f1" else 0
        return LINKS.get(item[0], 0)

    def link_counts(s, kinds):
        return counts(((place, i), place, late) for place, (item, slot, late) in enumerate(ORDER)
                      if slot == s for i in range(kinds(item)))

    ctx = ExitStack()
    with ctx:
        def sb(name, shape, dt=f32):
            return ctx.enter_context(nc.sbuf_tensor(name, shape, dt))

        def pb(name, shape, dt=f32):
            return ctx.enter_context(nc.psum_tensor(name, shape, dt))

        def sem(name):
            return ctx.enter_context(nc.semaphore(name))

        ident32 = sb("ident32", [P, P])
        ident16 = sb("ident16", [P, P], f16)
        identb = sb("identb", [P, P], bf16)
        neg_mask = sb("neg_mask", [P, NB, N], bf16)
        sel_row = sb("sel_row", [P, HEADS[2], N], f16)
        sel_col = sb("sel_col", [P, HEADS[2], P], f16)
        W = {k: sb(f"w_{k}", [P, 2, CT, C], f16) for k in ("h0", "q", "k", "v", "f1", "f2", "h2", "g", "h3")}
        W["s0"] = sb("w_s0", [P, 2, CT, P], f16)
        W["s2"] = sb("w_s2", [P, 2, CT, P], f16)
        rows = {k: sb(f"row_{k}", [P, C]) for k in ("g1", "b1", "g2", "b2", "fb2")}
        ffn_bias = sb("ffn_bias", [P, CT])

        S2 = range(SLOTS)
        xin = [sb(f"xin{s}", [P, NB, C]) for s in S2]
        xcur = [sb(f"xcur{s}", [P, NB, C]) for s in S2]
        xout = [sb(f"xout{s}", [P, NB, C]) for s in S2]
        za = [sb(f"za{s}", [P, NB, C]) for s in S2]
        zb = [sb(f"zb{s}", [P, NB, C]) for s in S2]
        xt = [sb(f"xt{s}", [P, 2, CT, N], f16) for s in S2]
        qk = [sb(f"qk{s}", [P, 2, 2, CT, N], f16) for s in S2]
        proj = [qk[s][:, :, 0] for s in S2]
        proj_k = [qk[s][:, :, 1] for s in S2]
        val = [sb(f"val{s}", [P, 2, NB, C], f16) for s in S2]
        s12 = [sb(f"s12_{s}", [P, N], f16) for s in S2]
        qk4 = [sb(f"qk4_{s}", [P, 2, CT, P // D1, N], f16) for s in S2]
        rowsum = [sb(f"rowsum{s}", [P, NB, HEADS[1]]) for s in S2]
        rinv = [sb(f"rinv{s}", [P, NB, HEADS[1]]) for s in S2]
        stats = [sb(f"stats{s}", [P, NB, 6]) for s in S2]
        moments = [sb(f"moments{s}", [P, NB, 2]) for s in S2]
        small = [sb(f"small{s}", [P, 8, NB]) for s in S2]

        relu_r = sb("relu_r", [P, RING, N])
        masked_r = sb("masked_r", [P, RING, N])
        low_r = sb("low_r", [P, RING])
        prob_r = sb("prob_r", [P, RING, N])
        split_r = sb("split_r", [P, RING, 2, N], f16)
        trans_r = sb("trans_r", [P, RING, 2, NB, P], f16)

        scores_ps = [pb(f"scores_ps{i}", [P, N]) for i in range(2)]
        trans_ps = [pb(f"trans_ps{i}", [P, 2, NB, P], f16) for i in range(2)]
        acc_ps = [pb(f"acc_ps{s}", [P, NB, C]) for s in S2]

        CREDIT = [8 + 256 * s for s in range(SLOTS)]

        def counted(name, table_of):
            found = []
            for s in range(SLOTS):
                table = table_of(s)
                found.append((sem(f"{name}{s}"), table, CREDIT[s] + sum(late for _, _, late in table.values())))
            return found

        scores_done = counted("scores_done", unit_counts)
        trans_done = counted("trans_done", unit_counts)
        layer_done = counted("layer_done", lambda s: unit_counts(
            s, lambda u: UNITS[u][2:4] == (HEADS[UNITS[u][0]] - 1, NB - 1)))
        dense_full = counted("dense_full", lambda s: item_counts("job", s))
        relu_done = counted("relu_done", lambda s: unit_counts(s, lambda u: LEAKY[UNITS[u][0]]))
        probs_done = counted("probs_done", unit_counts)
        evac_act = counted("evac_act", lambda s: unit_counts(s, lambda u: u % NB in ACT_EVAC))
        dense_hi = counted("dense_hi", lambda s: item_counts("job", s))
        elu_exp = counted("elu_exp", lambda s: item_counts("elu_min", s))
        masked_done = counted("masked_done", unit_counts)
        hi_done = counted("hi_done", unit_counts)
        evac_dve = counted("evac_dve", lambda s: unit_counts(s, lambda u: u % NB in DVE_EVAC))
        dense_lo = counted("dense_lo", lambda s: item_counts("job", s))
        elu_min = counted("elu_min", lambda s: item_counts("elu_min", s))
        applied = counted("applied", lambda s: item_counts("apply", s))
        dve_chain = counted("dve_chain", lambda s: link_counts(s, links))
        lo_done = counted("lo_done", unit_counts)
        affine_done = counted("affine_done", lambda s: item_counts("affine", s))
        x_loaded = [sem(f"x_loaded{s}") for s in S2]
        stacked = [sem(f"stacked{s}") for s in S2]
        out_stored = [sem(f"out_stored{s}") for s in S2]
        OUT_CREDIT = 16
        Q_PART = [c // 2 for c in range(COPIES)]
        K_PART = [c % 2 for c in range(COPIES)]
        STACKS = [(slice(0, 2), c, Q_PART[c]) for c in range(COPIES) if Q_PART[c] == K_PART[c]]
        STACKS += [(slice(w, w + 1), c, (Q_PART, K_PART)[w][c]) for c in range(COPIES) if Q_PART[c] != K_PART[c] for w in range(2)]
        STACK_DMAS = len(STACKS) * (P // D1)


        w_loaded = sem("w_loaded")
        ident_ready = sem("ident_ready")
        setup_pool = sem("setup_pool")
        setup_dve = sem("setup_dve")
        setup_pe = sem("setup_pe")
        dve_setup_chain = sem("dve_setup_chain")
        masking = sem("masking")
        credit_cell = sb("credit_cell", [P, 32])
        credit_dve = sb("credit_dve", [P, 16])

        stage_w = {k: buf[0][:, CT * half:CT * half + CT, :]
                   for buf, keys in ((xcur, ("h0", "q")), (xout, ("k", "v")), (za, ("f1", "f2")), (zb, ("h2", "h3")))
                   for half, k in enumerate(keys)}
        stage_d1 = zb[1][:, 0:CT, :]
        stage_d2 = zb[1][:, CT:2 * CT, :]
        stage_t1 = za[1][:, 0:CT, :]
        stage_t2 = za[1][:, CT:2 * CT, :]
        stage_g = xcur[1][:, 0:CT, :]
        stage_s0 = xcur[1][:, CT, :].rearrange("p (t n) -> p t n", t=CT)
        stage_s2 = xcur[1][:, CT + 1, :].rearrange("p (t n) -> p t n", t=CT)
        stage_a0 = xout[1][:, 0:2, :]
        stage_a2 = xout[1][:, 2, 0:C // 2]
        stage_scratch = xout[1][:, 3, :]
        stage_adj = masked_r[:, :, :].bitcast(i32)
        stage_flag = prob_r

        block = ctx.enter_context(nc.Block())

        def wait(eng, it, here, counter, slot, key):
            semaphore, table, _ = counter[slot]
            place, n, _ = table[key]
            if place > here:
                n -= len(table)
            eng.wait_ge(semaphore, it * len(table) + (n + CREDIT[slot]))

        def wait_unit(eng, it, here, counter, u):
            wait(eng, it, here, counter, UNITS[u][1], u)

        def last_user(it, active, u, depth):
            v = u - depth
            while v >= 0 and not active(UNITS[v][4]):
                v -= depth
            if v < 0 and isinstance(it, int) and it == 0:
                return None
            return v % len(UNITS)

        def wait_user(eng, it, here, active, counter, u, depth):
            v = last_user(it, active, u, depth)
            if v is not None:
                wait_unit(eng, it, here, counter, v)

        def wait_evac(eng, it, here, u):
            wait_unit(eng, it, here, evac_act if u % NB in ACT_EVAC else evac_dve, u)

        def turns(eng, run):
            run(0, lambda late: not late)
            with eng.Fori(1, TURNS) as it:
                run(it, lambda late: True)
            run(TURNS, lambda late: late)

        def stages(item):
            return [pipe[item[1] - lag] if item[1] >= lag else None for lag in (0, LAG_HI, LAG_T, LAG_PV)]

        def graph(it, late):
            return it - 1 if late else it

        def everywhere(key):
            return rows[key][:].unsqueeze(1).broadcast_to([P, NB, C])

        def w_view(w):
            return w.rearrange("(t p) n -> p t n", p=P)

        @block.sync
        def _(sp):
            for k, src in (("h0", gat_w), ("q", w_qkv[:, 0:C]), ("k", w_qkv[:, C:2 * C]), ("v", w_qkv[:, 2 * C:3 * C]),
                           ("f1", ffn_w1), ("f2", ffn_w2), ("h2", mh_w), ("h3", dot_w3)):
                sp.dma_start(stage_w[k], w_view(src)).then_inc(w_loaded, 16)
            sp.dma_start(stage_d1, w_view(dot_w1)).then_inc(w_loaded, 16)
            sp.dma_start(stage_d2, w_view(dot_w2)).then_inc(w_loaded, 16)
            for k, src in (("g1", ln1_g), ("b1", ln1_b), ("g2", ln2_g), ("b2", ln2_b), ("fb2", ffn_b2)):
                sp.dma_start(rows[k][:], src.rearrange("(o n) -> o n", o=1).broadcast_to([P, C])).then_inc(w_loaded, 16)
            sp.dma_start(ffn_bias[:], ffn_b1.rearrange("(t p) -> p t", p=P), allow_slow_non_contiguous=True).then_inc(w_loaded, 16)
            sp.dma_start(stage_a0, gat_a.rearrange("(t n) o -> o t n", t=2).broadcast_to([P, 2, C])).then_inc(w_loaded, 16)
            sp.dma_start(stage_a2, mh_a.rearrange("(o n) -> o n", o=1).broadcast_to([P, C // 2])).then_inc(w_loaded, 16)
            sp.dma_start(stage_adj, adj.rearrange("(b p) n -> p b n", p=P)).then_inc(w_loaded, 16)

            def load_x(g, s):
                sp.dma_start(xin[s][:], x[g * SLOTS + s].rearrange("(b p) c -> p b c", p=P)).then_inc(x_loaded[s], 16)

            for s in S2:
                load_x(0, s)

            def run(it, active):
                for here, (item, s, late) in enumerate(ORDER):
                    if not active(late):
                        continue
                    g = graph(it, late)
                    if item[0] == "load":
                        if not (isinstance(g, int) and g + 1 == TURNS):
                            wait(sp, it, here, applied, s, (0,))
                            load_x(g + 1, s)
                    elif item[0] == "stack":
                        j = GROUPS[GROUP_OF[1]].index(("k", CT - 1))
                        wait(sp, it, here, dense_lo, s, (GROUP_OF[1], j))
                        for h in range(P // D1):
                            for which, c, part in STACKS:
                                sp.dma_start(qk4[s][c * D1:(c + 1) * D1, which, :, h, :],
                                             qk[s][h * D1:(h + 1) * D1, part, which, :, :]).then_inc(stacked[s], 16)
                    elif item[0] == "store":
                        wait(sp, it, here, applied, s, (3,))
                        sp.dma_start(out[g * SLOTS + s].rearrange("(b p) c -> p b c", p=P), xout[s][:]).then_inc(out_stored[s], 16)

            run(0, lambda late: not late)
            with sp.Fori(1, TURNS - 1) as it:
                run(it, lambda late: True)
            run(TURNS - 1, lambda late: True)
            run(TURNS, lambda late: late)
            for s in S2:
                sp.wait_ge(out_stored[s], 16 * TURNS + OUT_CREDIT)

        @block.gpsimd
        def _(pool):
            nc.gpsimd.memset(ident32[:], 0.0).then_inc(setup_pool, 1)
            nc.gpsimd.memset(sel_row[:], 0.0).then_inc(setup_pool, 1)
            nc.gpsimd.memset(sel_col[:], 0.0).then_inc(setup_pool, 1)
            pool.wait_ge(setup_pool, 3)
            nc.gpsimd.affine_select(out=ident32[:], in_=ident32[:], compare_op=ALU.not_equal, fill=1.0, base=0,
                                    pattern=[[-1, P]], channel_multiplier=1).then_inc(ident_ready, 1)
            for n, (tile, at_row) in enumerate(((sel_row, 0), (sel_row, 32), (sel_col, 64), (sel_col, 96))):
                width = tile.shape[2]
                nc.gpsimd.affine_select(out=tile[:], in_=tile[:], compare_op=ALU.not_equal, fill=1.0,
                                        base=-at_row, pattern=[[-1, HEADS[2]], [0, width]],
                                        channel_multiplier=1).then_inc(setup_pool, 1)
                pool.wait_ge(setup_pool, 4 + n)
            for s in S2:
                nc.gpsimd.memset(credit_cell[:, s:s + 1], 0.0).then_inc(out_stored[s], OUT_CREDIT)
            for n, (semaphore, _, start) in enumerate([*lo_done, *affine_done]):
                nc.gpsimd.memset(credit_cell[:, 2 + n:3 + n], 0.0).then_inc(semaphore, start)

            def run(it, active):
                for here, (item, s, late) in enumerate(ORDER):
                    if item[0] == "step":
                        u = stages(item)[1]
                        if u is not None and active(UNITS[u][4]):
                            wait_unit(pool, it, here, hi_done, u)
                            wait_user(pool, it, here, active, trans_done, u, RING)
                            nc.gpsimd.tensor_tensor(split_r[:, u % RING, 1, :], prob_r[:, u % RING, :],
                                                    split_r[:, u % RING, 0, :], ALU.subtract).then_inc(lo_done[UNITS[u][1]][0], 1)
                    elif item[0] == "affine" and active(late):
                        if item[1] == 1:
                            wait(pool, it, here, applied, s, (1,))
                            ins = nc.gpsimd.tensor_tensor(zb[s][:], xout[s][:], everywhere("fb2"), ALU.add)
                        else:
                            wait(pool, it, here, applied, s, ("ffn",))
                            ins = nc.gpsimd.tensor_tensor(zb[s][:], zb[s][:], xcur[s][:], ALU.add)
                        ins.then_inc(affine_done[s][0], 1)

            turns(pool, run)

        @block.scalar
        def _(act):
            act.wait_ge(ident_ready, 1)
            for n, (semaphore, _, start) in enumerate([*relu_done, *probs_done, *evac_act, *dense_hi, *elu_exp]):
                nc.scalar.copy(credit_cell[:, 8 + n:9 + n], ident32[:, 0:1]).then_inc(semaphore, start)

            def dense(it, here, g, j, s):
                kind, n = GROUPS[g][j]
                bank = acc_ps[s][:, 2 * (j % 2):2 * (j % 2) + 2, :].rearrange("p a c -> p (a c)")
                wait(act, it, here, dense_full, s, (g, j))
                if kind == "xt":
                    ins = nc.scalar.copy(xt[s][:, 0, n, :], bank)
                elif kind in ("q", "k", "g"):
                    dst = proj_k if kind == "k" else proj
                    scale = {"q": QK_SCALE, "k": 1.0, "g": SLOPE}[kind] / WSCALE
                    ins = nc.scalar.activation(dst[s][:, 0, n, :], bank, ACT.Copy, scale=scale)
                elif kind in ("s0", "s2"):
                    ins = nc.scalar.activation(s12[s][:], bank, ACT.Copy, scale=1.0 / WSCALE)
                elif kind == "f1":
                    ins = nc.scalar.activation(za[s][:, 2 * n:2 * n + 2, :].rearrange("p a c -> p (a c)"), bank,
                                               ACT.Relu, bias=ffn_bias[:, n:n + 1], scale=1.0 / WSCALE)
                elif kind == "f2":
                    ins = nc.scalar.activation(za[s][:, 2 * n:2 * n + 2, :].rearrange("p a c -> p (a c)"), bank,
                                               ACT.Copy, scale=1.0 / WSCALE)
                else:
                    ins = nc.scalar.activation(val[s][:, 0, 2 * n:2 * n + 2, :].rearrange("p a c -> p (a c)"), bank,
                                               ACT.Copy, scale=1.0 / WSCALE)
                ins.then_inc(dense_hi[s][0], 1)

            def relu(it, here, active, u):
                wait_unit(act, it, here, scores_done, u)
                wait_user(act, it, here, active, masked_done, u, RING)
                nc.scalar.activation(relu_r[:, u % RING, :], scores_ps[u % 2][:], ACT.Relu,
                                     scale=1.0 / SLOPE - 1.0).then_inc(relu_done[UNITS[u][1]][0], 1)

            def probs(it, here, active, u):
                layer, s, h, b, _ = UNITS[u]
                wait_unit(act, it, here, masked_done, u)
                wait_user(act, it, here, active, lo_done, u, RING)
                nc.scalar.activation(prob_r[:, u % RING, :], masked_r[:, u % RING, :], ACT.Exp,
                                     bias=low_r[:, u % RING:u % RING + 1], scale=-1.0,
                                     accum_out=rowsum[s][:, b, h:h + 1]).then_inc(probs_done[s][0], 1)

            def run(it, active):
                for here, (item, s, late) in enumerate(ORDER):
                    if item[0] == "step":
                        new, _, old, _ = stages(item)
                        p = pipe[item[1] - LAG_P] if item[1] >= LAG_P else None
                        if new is not None and active(UNITS[new][4]) and LEAKY[UNITS[new][0]]:
                            relu(it, here, active, new)
                        if old is not None and active(UNITS[old][4]) and old % NB in ACT_EVAC:
                            wait_unit(act, it, here, trans_done, old)
                            nc.scalar.copy(trans_r[:, old % RING], trans_ps[old % 2][:]).then_inc(evac_act[UNITS[old][1]][0], 1)
                        if p is not None and active(UNITS[p][4]):
                            probs(it, here, active, p)
                    elif not active(late):
                        continue
                    elif item[0] == "job":
                        dense(it, here, item[1], item[2], s)
                    elif item[0] == "elu_min":
                        wait(act, it, here, elu_min, s, item[1:])
                        nc.scalar.activation(zb[s][:], zb[s][:], ACT.Exp).then_inc(elu_exp[s][0], 1)

            turns(act, run)

        @block.vector
        def _(dve):
            setup = [0]

            def after(ins):
                setup[0] += 1
                ins.then_inc(dve_setup_chain, 1)
                dve.wait_ge(dve_setup_chain, setup[0])

            for n, (semaphore, _, start) in enumerate([*masked_done, *hi_done, *evac_dve, *dense_lo, *elu_min, *applied,
                                                       *dve_chain]):
                nc.vector.memset(credit_dve[:, n:n + 1], 0.0).then_inc(semaphore, start)
            dve.wait_ge(w_loaded, 16 * 19)
            dve.wait_ge(ident_ready, 1)
            nc.vector.tensor_copy(ident16[:], ident32[:])
            after(nc.vector.tensor_copy(identb[:], ident32[:]))
            after(nc.vector.tensor_scalar(stage_flag[:], stage_adj, 0.0, 1.0, ALU.is_gt, ALU.subtract))
            after(nc.vector.tensor_scalar(neg_mask[:], stage_flag[:], MASKED, None, ALU.mult))

            def split_weight(dst, src, scale):
                after(nc.vector.tensor_scalar(dst[:, 0], src, scale, None, ALU.mult))
                after(nc.vector.scalar_tensor_tensor(out=dst[:, 1], in0=src, scalar=scale, in1=dst[:, 0],
                                                     op0=ALU.mult, op1=ALU.subtract))

            for key, stage_s, heads, stage_src in (("s0", stage_s0, 1, stage_w["h0"]), ("s2", stage_s2, HEADS[2], stage_w["h2"])):
                after(nc.vector.memset(stage_s, 0.0))
                width = C // heads
                for h in range(heads):
                    for side in range(2):
                        for t in range(CT):
                            a = stage_a0[:, side, :] if heads == 1 else stage_a2[:, side * width:(side + 1) * width]
                            col = 64 * side + h
                            after(nc.vector.tensor_tensor_reduce(
                                out=stage_scratch[:, 0:width], in0=stage_src[:, t, h * width:(h + 1) * width], in1=a,
                                scale=1.0, scalar=0.0, op0=ALU.mult, op1=ALU.add, accum_out=stage_s[:, t, col:col + 1]))
                for side in range(2):
                    after(nc.vector.tensor_copy(stage_s[:, :, 64 * side + 32:64 * side + 32 + heads],
                                                stage_s[:, :, 64 * side:64 * side + heads]))
                split_weight(W[key], stage_s, WSCALE * SLOPE)
            for k in ("h0", "q", "k", "v", "f1", "f2", "h2", "h3"):
                split_weight(W[k], stage_w[k], WSCALE)
            dve.wait_ge(setup_pe, 1)
            nc.vector.tensor_copy(stage_t1, acc_ps[0][:, 0:2, :])
            nc.vector.tensor_copy(stage_t2, acc_ps[0][:, 2:4, :]).then_inc(setup_dve, 1)
            dve.wait_ge(setup_pe, 2)
            after(nc.vector.tensor_copy(stage_g, acc_ps[1][:, 0:2, :]))
            split_weight(W["g"], stage_g, WSCALE)
            nc.vector.memset(credit_dve[:, 15:16], 0.0).then_inc(setup_dve, 1)

            done_links = [0] * SLOTS

            def link(s, ins):
                done_links[s] += 1
                ins.then_inc(dve_chain[s][0], 1)

            def own(it, s):
                semaphore, table, _ = dve_chain[s]
                dve.wait_ge(semaphore, it * len(table) + (done_links[s] + CREDIT[s]))

            def dense(it, here, g, j, s):
                kind, n = GROUPS[g][j]
                bank = acc_ps[s][:, 2 * (j % 2):2 * (j % 2) + 2, :].rearrange("p a c -> p (a c)")
                wait(dve, it, here, dense_hi, s, (g, j))

                def lo(dst, hi, scale):
                    return nc.vector.scalar_tensor_tensor(out=dst, in0=bank, scalar=scale, in1=hi,
                                                          op0=ALU.mult, op1=ALU.subtract)

                if kind == "xt":
                    ins = lo(xt[s][:, 1, n, :], xt[s][:, 0, n, :], 1.0)
                elif kind in ("q", "k", "g"):
                    dst = proj_k if kind == "k" else proj
                    scale = {"q": QK_SCALE, "k": 1.0, "g": SLOPE}[kind] / WSCALE
                    ins = lo(dst[s][:, 1, n, :], dst[s][:, 0, n, :], scale)
                elif kind in ("s0", "s2"):
                    for quadrant in (1, 3):
                        r = slice(32 * quadrant, 32 * quadrant + 32)
                        ins = nc.vector.scalar_tensor_tensor(out=s12[s][r, :], in0=bank[r, :], scalar=1.0 / WSCALE,
                                                             in1=s12[s][r, :], op0=ALU.mult, op1=ALU.subtract)
                elif kind == "f1":
                    hid = za[s][:, 2 * n:2 * n + 2, :].rearrange("p a c -> p (a c)")
                    link(s, nc.vector.tensor_copy(proj[s][:, 0, n, :], hid))
                    own(it, s)
                    ins = nc.vector.tensor_tensor(proj[s][:, 1, n, :], hid, proj[s][:, 0, n, :], ALU.subtract)
                elif kind == "f2":
                    wait(dve, it, here, affine_done, s, (1,))
                    ins = nc.vector.tensor_tensor(za[s][:, 2 * n:2 * n + 2, :], za[s][:, 2 * n:2 * n + 2, :],
                                                  zb[s][:, 2 * n:2 * n + 2, :], ALU.add)
                else:
                    v = [val[s][:, p, 2 * n:2 * n + 2, :].rearrange("p a c -> p (a c)") for p in range(2)]
                    ins = lo(v[1], v[0], 1.0 / WSCALE)
                ins.then_inc(dense_lo[s][0], 1)

            NORM_SRC = {0: za, 1: za, 2: za, 3: za, "ffn": za, "out1": zb}
            NORM_DST = {0: xcur, 1: xout, 2: xcur, 3: xout, "ffn": zb, "out1": xcur}
            VAR, HALF, SQUARE, Y0, Y1 = range(5)

            def finish(it, here, item, s, late):
                kind = item[0]
                col = [small[s][:, n, :] for n in range(5)]
                if kind == "recip":
                    heads = HEADS[item[1]]
                    last = max(u for u in layer_done[s][1] if UNITS[u][0] == item[1])
                    wait(dve, it, here, layer_done, s, last)
                    link(s, nc.vector.reciprocal(rinv[s][:, :, 0:heads], rowsum[s][:, :, 0:heads]))
                elif kind == "divide":
                    heads = HEADS[item[1]]
                    own(it, s)
                    link(s, nc.vector.tensor_tensor(
                        za[s][:].rearrange("p b (h d) -> p b h d", h=heads),
                        acc_ps[s][:].rearrange("p b (h d) -> p b h d", h=heads),
                        rinv[s][:, :, 0:heads].unsqueeze(3).broadcast_to([P, NB, heads, C // heads]), ALU.mult))
                elif kind == "elu_min":
                    own(it, s)
                    nc.vector.tensor_scalar(zb[s][:], za[s][:], 0.0, None, ALU.min).then_inc(elu_min[s][0], 1)
                    if item[1] == 0:
                        dve.wait_ge(x_loaded[s], graph(it, late) * 16 + 16)
                    old = xin if item[1] == 0 else xcur
                    link(s, nc.vector.scalar_tensor_tensor(out=za[s][:], in0=za[s][:], scalar=0.0, in1=old[s][:],
                                                           op0=ALU.max, op1=ALU.add))
                elif kind == "elu_add":
                    own(it, s)
                    wait(dve, it, here, elu_exp, s, (item[1],))
                    link(s, nc.vector.scalar_tensor_tensor(out=za[s][:], in0=zb[s][:], scalar=-1.0, in1=za[s][:],
                                                           op0=ALU.add, op1=ALU.add))
                elif kind == "residual":
                    own(it, s)
                    if item[1] == 3:
                        ins = nc.vector.scalar_tensor_tensor(out=za[s][:], in0=za[s][:], scalar=0.0, in1=xcur[s][:],
                                                             op0=ALU.max, op1=ALU.add)
                    else:
                        ins = nc.vector.tensor_tensor(za[s][:], za[s][:], xcur[s][:], ALU.add)
                    link(s, ins)
                elif kind == "stats":
                    _, b, which = item
                    if b == 0 and which == "ffn":
                        wait(dve, it, here, dense_lo, s, (FFN, len(GROUPS[FFN]) - 1))
                    elif b == 0 and which == "out1":
                        wait(dve, it, here, affine_done, s, (2,))
                    elif b == 0:
                        own(it, s)
                    link(s, nc.vector.bn_stats(stats[s][:, b, :], NORM_SRC[which][s][:, b, :]))
                elif kind == "aggregate":
                    own(it, s)
                    dve.sem_inc(masking, 1)
                    for b in range(NB):
                        ins = nc.vector.bn_aggr(moments[s][:, b, :], stats[s][:, b, :])
                    link(s, ins)
                elif kind == "add_eps":
                    own(it, s)
                    link(s, nc.vector.tensor_scalar(col[VAR], moments[s][:, :, 1], EPS, None, ALU.add))
                elif kind == "seed":
                    own(it, s)
                    link(s, nc.vector.tensor_scalar(col[Y0].bitcast(i32), col[VAR].bitcast(i32), -0.5, RSQRT_SEED,
                                                    ALU.mult, ALU.add))
                elif kind == "newton":
                    _, n, part, _ = item
                    y, z = (Y0, Y1) if n % 2 == 0 else (Y1, Y0)
                    own(it, s)
                    if part == 0:
                        ins = nc.vector.scalar_tensor_tensor(out=col[SQUARE], in0=col[y], scalar=-0.5, in1=col[y],
                                                             op0=ALU.mult, op1=ALU.mult)
                    elif part == 1:
                        ins = nc.vector.tensor_tensor(col[HALF], col[SQUARE], col[VAR], ALU.mult)
                    else:
                        ins = nc.vector.scalar_tensor_tensor(out=col[z], in0=col[HALF], scalar=1.5, in1=col[y],
                                                             op0=ALU.add, op1=ALU.mult)
                    link(s, ins)
                elif kind == "gain":
                    which = item[1]
                    own(it, s)
                    for b in range(NB):
                        ins = nc.vector.scalar_tensor_tensor(
                            out=zb[s][:, b, :], in0=za[s][:, b, :], scalar=moments[s][:, b, 0:1],
                            in1=rows[{1: "g1", "ffn": "g2"}[which]][:], op0=ALU.subtract, op1=ALU.mult)
                    link(s, ins)
                elif kind == "apply":
                    which = item[1]
                    own(it, s)
                    if which == 1:
                        dve.wait_ge(out_stored[s], graph(it, late) * 16 + OUT_CREDIT)
                    for b in range(NB):
                        dst = NORM_DST[which][s][:, b, :]
                        scale = small[s][:, Y1, b:b + 1]
                        if which in (1, "ffn"):
                            ins = nc.vector.scalar_tensor_tensor(
                                out=dst, in0=zb[s][:, b, :], scalar=scale, in1=rows[{1: "b1", "ffn": "b2"}[which]][:],
                                op0=ALU.mult, op1=ALU.add)
                        else:
                            ins = nc.vector.tensor_scalar(dst, NORM_SRC[which][s][:, b, :], moments[s][:, b, 0:1], scale,
                                                          ALU.subtract, ALU.mult)
                    ins.then_inc(applied[s][0], 1)

            def masked(it, here, active, u):
                layer, s, h, b, _ = UNITS[u]
                wait_user(dve, it, here, active, probs_done, u, RING)
                if LEAKY[layer]:
                    wait(dve, it, here, relu_done, s, u)
                    second = relu_r[:, u % RING, :]
                else:
                    wait(dve, it, here, scores_done, s, u)
                    second = neg_mask[:, b, :]
                dve.sem_inc(masking, 1)
                nc.vector.tensor_tensor_reduce(out=masked_r[:, u % RING, :], in0=scores_ps[u % 2][:], in1=second,
                                               scale=-1.0, scalar=BIG, op0=ALU.add, op1=ALU.min,
                                               accum_out=low_r[:, u % RING:u % RING + 1]).then_inc(masked_done[s][0], 1)

            def run(it, active):
                for s in S2:
                    done_links[s] = 0
                for here, (item, s, late) in enumerate(ORDER):
                    if item[0] == "step":
                        new, middle, old, _ = stages(item)
                        if new is not None and active(UNITS[new][4]):
                            masked(it, here, active, new)
                        if old is not None and active(UNITS[old][4]) and old % NB in DVE_EVAC:
                            wait_unit(dve, it, here, trans_done, old)
                            nc.vector.tensor_copy(trans_r[:, old % RING], trans_ps[old % 2][:]).then_inc(evac_dve[UNITS[old][1]][0], 1)
                        if middle is not None and active(UNITS[middle][4]):
                            u = middle
                            wait_unit(dve, it, here, probs_done, u)
                            wait_user(dve, it, here, active, trans_done, u, RING)
                            nc.vector.tensor_copy(split_r[:, u % RING, 0, :], prob_r[:, u % RING, :]).then_inc(hi_done[UNITS[u][1]][0], 1)
                    elif not active(late):
                        done_links[s] += links(item)
                    elif item[0] == "job":
                        dense(it, here, item[1], item[2], s)
                    else:
                        before = done_links[s]
                        finish(it, here, item, s, late)
                        assert done_links[s] == before + links(item)

            turns(dve, run)

        @block.tensor
        def _(pe):
            pe.wait_ge(ident_ready, 1)
            pe.wait_ge(w_loaded, 16 * 19)
            for half, src in enumerate((stage_d1, stage_d2)):
                for tf in range(CT):
                    for tc in range(CT):
                        ins = nc.tensor.transpose(acc_ps[0][:, 2 * half + tf, tc * P:(tc + 1) * P],
                                                  src[:, tc, tf * P:(tf + 1) * P], ident32[:])
            ins.then_inc(setup_pe, 1)
            pe.wait_ge(setup_dve, 1)
            for tc in range(CT):
                for tf in range(CT):
                    ins = nc.tensor.matmul(acc_ps[1][:, tc, :], stage_t1[:, tf, tc * P:(tc + 1) * P], stage_t2[:, tf, :],
                                           start=(tf == 0), stop=(tf == CT - 1))
            ins.then_inc(setup_pe, 1)
            for semaphore, _, start in [*scores_done, *trans_done, *layer_done, *dense_full]:
                nc.tensor.transpose(scores_ps[0][:, 0:P], ident32[:], ident32[:]).then_inc(semaphore, start)
            pe.wait_ge(setup_dve, 2)
            pe.wait_ge(setup_pool, 7)

            TERMS = [(0, 0), (0, 1), (1, 0)]

            def dense(it, here, g, j, s, late):
                kind, n = GROUPS[g][j]
                bank = acc_ps[s][:, 2 * (j % 2):2 * (j % 2) + 2, :]
                flat = bank.rearrange("p a c -> p (a c)")
                if j == 0:
                    if g == 0:
                        pe.wait_ge(x_loaded[s], graph(it, late) * 16 + 16)
                        wait(pe, it, here, applied, s, (3,))
                    elif g == FFN:
                        wait(pe, it, here, applied, s, (1,))
                    else:
                        wait(pe, it, here, applied, s, ({1: 0, 3: "out1", 4: 2}[g],))
                if j >= 2:
                    wait(pe, it, here, dense_lo, s, (g, j - 2))
                if j == 2 or (kind == "f2" and n == 0):
                    wait(pe, it, here, dense_lo, s, (g, j - 1))
                if kind == "xt":
                    src = {0: xin, FFN: xout}.get(g, xcur)
                    for b in range(NB):
                        ins = nc.tensor.transpose(flat[:, b * P:(b + 1) * P], src[s][:, b, n * P:(n + 1) * P], ident32[:])
                elif kind in ("q", "k", "g", "s0", "s2", "f1"):
                    ops = [(wp, xp, t) for t in range(CT) for wp, xp in TERMS]
                    for i, (wp, xp, t) in enumerate(ops):
                        ins = nc.tensor.matmul(flat, W[kind][:, wp, t, n * P:(n + 1) * P], xt[s][:, xp, t, :],
                                               start=(i == 0), stop=(i == len(ops) - 1))
                else:
                    left = proj if kind == "f2" else xt
                    ops = [(xp, wp, t) for t in range(CT) for xp, wp in TERMS]
                    for half in range(2):
                        b = 2 * n + half
                        for i, (xp, wp, t) in enumerate(ops):
                            ins = nc.tensor.matmul(bank[:, half, :], left[s][:, xp, t, b * P:(b + 1) * P],
                                                   W[kind][:, wp, t, :], start=(i == 0), stop=(i == len(ops) - 1))
                ins.then_inc(dense_full[s][0], 1)

            def scores(it, here, active, u):
                layer, s, h, b, late = UNITS[u]
                ps = scores_ps[u % 2][:]
                q = slice(b * P, (b + 1) * P)
                if h == 0 and b == 0:
                    g = GROUP_OF[layer]
                    wait(pe, it, here, dense_lo, s, (g, len(GROUPS[g]) - 1))
                    if layer == 1:
                        pe.wait_ge(stacked[s], graph(it, late) * (16 * STACK_DMAS) + 16 * STACK_DMAS)
                wait_user(pe, it, here, active, masked_done, u, 2)
                if layer == 1:
                    t, hq = divmod(h, P // D1)
                    ops = [(qk4[s][:, 0, t, hq, q], qk4[s][:, 1, t, hq, :])]
                elif layer == 3:
                    ops = [(proj[s][:, gp, t, q], xt[s][:, xp, t, :]) for t in range(CT) for gp, xp in TERMS]
                else:
                    ops = [(s12[s][:, q], sel_row[:, h, :]), (sel_col[:, h, :], s12[s][:])]
                if layer != 1:
                    ops.append((identb[:], neg_mask[:, b, :]))
                for i, (left, right) in enumerate(ops):
                    ins = nc.tensor.matmul(ps, left, right, start=(i == 0), stop=(i == len(ops) - 1))
                ins.then_inc(scores_done[s][0], 1)

            def transposes(it, here, active, u):
                wait_unit(pe, it, here, lo_done, u)
                before = last_user(it, active, u, 2)
                if before is not None:
                    wait_evac(pe, it, here, before)
                for part in range(2):
                    for jb in range(NB):
                        ins = nc.tensor.transpose(trans_ps[u % 2][:, part, jb, :],
                                                  split_r[:, u % RING, part, jb * P:(jb + 1) * P], ident16[:])
                ins.then_inc(trans_done[UNITS[u][1]][0], 1)

            def values(it, here, u):
                layer, s, h, b, _ = UNITS[u]
                width = C // HEADS[layer]
                cols = slice(h * width, (h + 1) * width)
                wait_evac(pe, it, here, u)
                ops = [(pp, vp, jb) for jb in range(NB) for pp, vp in TERMS]
                for i, (pp, vp, jb) in enumerate(ops):
                    ins = nc.tensor.matmul(acc_ps[s][:, b, cols], trans_r[:, u % RING, pp, jb, :], val[s][:, vp, jb, cols],
                                           start=(i == 0), stop=(i == len(ops) - 1))
                if u in layer_done[s][1]:
                    ins.then_inc(layer_done[s][0], 1)

            def run(it, active):
                for here, (item, s, late) in enumerate(ORDER):
                    if item[0] == "step":
                        new, _, old, oldest = stages(item)
                        if new is not None and active(UNITS[new][4]):
                            scores(it, here, active, new)
                        if old is not None and active(UNITS[old][4]):
                            transposes(it, here, active, old)
                        if oldest is not None and active(UNITS[oldest][4]):
                            values(it, here, oldest)
                    elif item[0] == "job" and active(late):
                        dense(it, here, item[1], item[2], s, late)

            turns(pe, run)


_INS = ['x', 'adj', 'L0_gnn_W', 'L0_gnn_a', 'L1_gnn_w_qkv', 'L1_gnn_ln1_g', 'L1_gnn_ln1_b', 'L1_gnn_ln2_g',
        'L1_gnn_ln2_b', 'L1_gnn_w1', 'L1_gnn_b1', 'L1_gnn_w2', 'L1_gnn_b2', 'L2_gnn_W', 'L2_gnn_a',
        'L3_gnn_W1', 'L3_gnn_W2', 'L3_gnn_W3']
_OUT = ((32, 512, 256), 'float32')


def kernel(**inputs):
    import numpy as _np
    import concourse.bacc as _bacc
    from concourse import mybir as _mybir
    from concourse.bass_utils import run_bass_kernel_spmd as _run

    nc = _bacc.Bacc("TRN2", target_bir_lowering=False, num_devices=1)
    arrays, args = {}, []
    for name in _INS:
        a = _np.ascontiguousarray(inputs[name])
        arrays[f"in_{name}_dram"] = a
        args.append(nc.dram_tensor(f"in_{name}_dram", a.shape, _mybir.dt.from_np(a.dtype), kind="ExternalInput").ap())
    shape, dtype = _OUT
    args.append(nc.dram_tensor("out_dram", shape, _mybir.dt.from_np(_np.dtype(dtype)), kind="ExternalOutput").ap())
    graph_layers_kernel(nc, *args)
    r = _run(nc, [arrays], core_ids=[0])
    return r.results[0]["out_dram"]
```

```python
import concourse.bass as bass
from concourse import mybir
from contextlib import ExitStack


def graph_layers_kernel(
    nc: bass.Bass,
    x: bass.AP,
    adj: bass.AP,
    gat_w: bass.AP,
    gat_a: bass.AP,
    w_qkv: bass.AP,
    ln1_g: bass.AP,
    ln1_b: bass.AP,
    ln2_g: bass.AP,
    ln2_b: bass.AP,
    ffn_w1: bass.AP,
    ffn_b1: bass.AP,
    ffn_w2: bass.AP,
    ffn_b2: bass.AP,
    mh_w: bass.AP,
    mh_a: bass.AP,
    dot_w1: bass.AP,
    dot_w2: bass.AP,
    dot_w3: bass.AP,
    out: bass.AP,
):
    f32 = mybir.dt.float32
    f16 = mybir.dt.float16
    bf16 = mybir.dt.bfloat16
    i32 = mybir.dt.int32
    ALU = mybir.AluOpType
    ACT = mybir.ActivationFunctionType

    P = 128
    B, N, C = x.shape
    NB = N // P
    CT = C // P
    SLOTS = 2
    TURNS = B // SLOTS
    WSCALE = 64.0
    SLOPE = 0.2
    EPS = 1e-5
    MASKED = 1e30
    BIG = 3e38
    QK_SCALE = 32.0 ** -0.5
    RSQRT_SEED = float(0x5F3759DF)
    HEADS = [1, 8, 4, 1]
    LAYERS = len(HEADS)
    LEAKY = [True, False, True, True]
    D1 = C // HEADS[1]
    STACK = [(0, 0), (0, 1), (1, 0)]

    TIMES = ({'group0': 25.64, 'layer0': 24.82, 'finish0': 58.42, 'group1': 26.43, 'layer1': 65.28, 'finish1': 14.79, 'group2': 6.55, 'normffn': 9.99, 'normout1': 24.33, 'group3': 11.54, 'layer2': 43.03, 'finish2': 13.79, 'group4': 18.29, 'layer3': 32.4, 'finish3': 26.65}, {'group0': 20.72, 'layer0': 16.4, 'finish0': 23.95, 'group1': 26.43, 'layer1': 133.84, 'finish1': 19.21, 'group2': 5.98, 'normffn': 8.88, 'normout1': 20.56, 'group3': 7.18, 'layer2': 41.77, 'finish2': 16.9, 'group4': 18.29, 'layer3': 24.52, 'finish3': 26.65})
    FILL = 31.19
    OFFSET = 0.854
    RING = 4
    TRING = 8
    LAG_HI, LAG_T, LAG_PV = (1, 3, 7)
    LAG_P = 1
    ACT_HI = ((), (1, 3), (), ())

    GROUPS = [
        [("xt", 0), ("xt", 1), ("h0", 0), ("h0", 1), ("s0", 0)],
        [("xt", 0), ("xt", 1), ("q", 0), ("q", 1), ("k", 0), ("k", 1), ("v", 0), ("v", 1)],
        [("xt", 0), ("xt", 1), ("f1", 0), ("f1", 1), ("f2", 0), ("f2", 1)],
        [("xt", 0), ("xt", 1), ("h2", 0), ("h2", 1), ("s2", 0)],
        [("xt", 0), ("xt", 1), ("g", 0), ("g", 1), ("h3", 0), ("h3", 1)],
    ]
    GROUP_OF = [0, 1, 3, 4]
    FFN = 2

    NORM = [("stats", b) for b in range(NB)] + [("aggregate",), ("add_eps",), ("seed",), ("product",)] \
        + [("newton", n, part) for n in range(3) for part in range(2)]
    GAINED = (1, "ffn")

    def norm(which):
        return [(*item, which) for item in NORM] + [("gain" if which in GAINED else "shift", which), ("apply", which)]

    def finish(layer):
        middle = {0: ["elu_sum", "elu_add"], 1: ["residual"], 2: ["elu_min", "elu_add"], 3: ["residual"]}[layer]
        return [("recip", layer), ("divide", layer)] + [(kind, layer) for kind in middle] + norm(layer)

    def group(g):
        return [("job", g, j) for j in range(len(GROUPS[g]))]

    def units(layer):
        return [("unit", layer, h, b) for h in range(HEADS[layer]) for b in range(NB)]

    PHASES = [("group0", group(0)), ("layer0", units(0)), ("finish0", finish(0) + [("load",)]),
              ("group1", group(1)[:6] + [("stack",)] + group(1)[6:]), ("layer1", units(1)), ("finish1", finish(1) + [("affine", 1), ("affine", 2)]),
              ("group2", group(FFN)), ("normffn", norm("ffn")), ("normout1", norm("out1")),
              ("group3", group(3)), ("layer2", units(2)), ("finish2", finish(2)),
              ("group4", group(4)), ("layer3", units(3)), ("finish3", finish(3) + [("store",)])]

    SPAN = sum(TIMES[0].values())
    timed = []
    for s in range(SLOTS):
        t = s * SPAN * OFFSET
        scale = SPAN / sum(TIMES[s].values())
        for phase, items in PHASES:
            length = TIMES[s][phase] * scale
            fill = min(FILL, length / 2) if phase.startswith("layer") else 0.0
            for n, item in enumerate(items):
                when = t + fill / 2 + (length - fill) * n / len(items)
                timed.append((when % SPAN, s, len(timed), item, when >= SPAN))
            t += length
    timed.sort()
    ORDER = []
    pipe = []
    order_units = []
    for _, s, _, item, late in timed:
        if item[0] == "unit":
            order_units.append((item[1], s, item[2], item[3], late))
            pipe.append(len(order_units) - 1)
            ORDER.append((("step", len(pipe) - 1), s, late))
            continue
        if item[0] == "recip":
            last = max((n for n, u in enumerate(order_units) if u[0] == item[1] and u[1] == s), default=None)
            while last is not None and len(pipe) - 1 < pipe.index(last) + LAG_PV:
                pipe.append(None)
                ORDER.append((("step", len(pipe) - 1), s, False))
        ORDER.append((item, s, late))
    while any(u is not None for u in pipe[-LAG_PV:]):
        pipe.append(None)
        ORDER.append((("step", len(pipe) - 1), 0, False))
    UNITS = order_units
    assert len(UNITS) % RING == 0 and len(UNITS) % TRING == 0

    def counts(items):
        return {key: (place, n + 1, late) for n, (key, place, late) in enumerate(items)}

    def item_counts(kind, s):
        return counts((item[1:], place, late) for place, (item, slot, late) in enumerate(ORDER)
                      if item[0] == kind and slot == s)

    STEP_PLACE = {pipe[item[1]]: place for place, (item, _, _) in enumerate(ORDER)
                  if item[0] == "step" and pipe[item[1]] is not None}

    def hi_by_act(u):
        return UNITS[u][3] in ACT_HI[UNITS[u][0]]

    def unit_counts(s, of=lambda u: True):
        return counts((u, STEP_PLACE[u], UNITS[u][4]) for u in range(len(UNITS)) if UNITS[u][1] == s and of(u))

    BY_ACT = [("divide", 0), ("divide", 3)] + [("apply", which) for which in (0, "out1", 2, 3)]

    LINKS = {"recip": 1, "divide": 1, "elu_min": 1, "elu_sum": 1, "elu_add": 1, "residual": 1, "stats": 1, "aggregate": 1,
             "add_eps": 1, "seed": 1, "product": 1, "newton": 1, "gain": 1}

    def links(item):
        if item[0] == "job":
            return 1 if GROUPS[item[1]][item[2]][0] == "f1" else 0
        if item in BY_ACT:
            return 0
        if item == ("apply", "ffn"):
            return 1
        return LINKS.get(item[0], 0)

    def link_counts(s, kinds):
        return counts(((place, i), place, late) for place, (item, slot, late) in enumerate(ORDER)
                      if slot == s for i in range(kinds(item)))

    ctx = ExitStack()
    with ctx:
        def sb(name, shape, dt=f32):
            return ctx.enter_context(nc.sbuf_tensor(name, shape, dt))

        def pb(name, shape, dt=f32):
            return ctx.enter_context(nc.psum_tensor(name, shape, dt))

        def sem(name):
            return ctx.enter_context(nc.semaphore(name))

        ident32 = sb("ident32", [P, P])
        identb = sb("identb", [P, P], bf16)
        neg_mask = sb("neg_mask", [P, NB, N], bf16)
        sel_row = sb("sel_row", [P, HEADS[2], N], f16)
        sel_col = sb("sel_col", [P, HEADS[2], P], f16)
        W = {k: sb(f"w_{k}", [P, 2, CT, C], f16) for k in ("h0", "q", "k", "v", "f1", "f2", "h2", "g", "h3")}
        W["s0"] = sb("w_s0", [P, 2, CT, P], f16)
        W["s2"] = sb("w_s2", [P, 2, CT, P], f16)
        rows = {k: sb(f"row_{k}", [P, C]) for k in ("g1", "b1", "g2", "b2", "fb2")}
        ffn_bias = sb("ffn_bias", [P, CT])

        S2 = range(SLOTS)
        xin = [sb(f"xin{s}", [P, NB, C]) for s in S2]
        xcur = [sb(f"xcur{s}", [P, NB, C]) for s in S2]
        xout = [sb(f"xout{s}", [P, NB, C]) for s in S2]
        za = [sb(f"za{s}", [P, NB, C]) for s in S2]
        zb = [sb(f"zb{s}", [P, NB, C]) for s in S2]
        xt = [sb(f"xt{s}", [P, 2, CT, N], f16) for s in S2]
        qk = [sb(f"qk{s}", [P, 4, CT, N], f16) for s in S2]
        proj = [qk[s][:, 0:2] for s in S2]
        proj_k = [qk[s][:, 2:4] for s in S2]
        val = [sb(f"val{s}", [P, 2, NB, C], f16) for s in S2]
        s12 = [sb(f"s12_{s}", [P, N], f16) for s in S2]
        stack = [sb(f"stack{s}", [len(STACK) * D1, P // D1, 2, CT, N], f16) for s in S2]
        rowsum = [sb(f"rowsum{s}", [P, NB, HEADS[1]]) for s in S2]
        rinv = [sb(f"rinv{s}", [P, NB, HEADS[1]]) for s in S2]
        stats = [sb(f"stats{s}", [P, NB, 6]) for s in S2]
        moments = [sb(f"moments{s}", [P, NB, 2]) for s in S2]
        small = [sb(f"small{s}", [P, 8, NB]) for s in S2]

        relu_r = sb("relu_r", [P, RING, N])
        masked_r = sb("masked_r", [P, RING, N])
        low_r = sb("low_r", [P, RING])
        prob_r = sb("prob_r", [P, RING, N])
        split_r = sb("split_r", [P, TRING, 2, N], f16)
        trans_r = sb("trans_r", [P, TRING, 2, NB, P], f16)

        scores_ps = [pb(f"scores_ps{i}", [P, N]) for i in range(RING)]
        acc_ps = [pb(f"acc_ps{s}", [P, NB, C]) for s in S2]

        CREDIT = [8 + 256 * s for s in range(SLOTS)]

        def counted(name, table_of):
            found = []
            for s in range(SLOTS):
                table = table_of(s)
                found.append((sem(f"{name}{s}"), table, CREDIT[s] + sum(late for _, _, late in table.values())))
            return found

        scores_done = counted("scores_done", unit_counts)
        values_done = counted("values_done", unit_counts)
        dense_full = counted("dense_full", lambda s: item_counts("job", s))
        relu_done = counted("relu_done", lambda s: unit_counts(s, lambda u: LEAKY[UNITS[u][0]]))
        probs_done = counted("probs_done", unit_counts)
        hi_act = counted("hi_act", lambda s: unit_counts(s, hi_by_act))
        dense_hi = counted("dense_hi", lambda s: item_counts("job", s))
        elu_exp = counted("elu_exp", lambda s: item_counts("elu_min", s))
        divided = counted("divided", lambda s: counts(
            (item[1:], place, late) for place, (item, slot, late) in enumerate(ORDER)
            if slot == s and item[0] == "divide" and item in BY_ACT))
        applied = counted("applied", lambda s: counts(
            (item[1:], place, late) for place, (item, slot, late) in enumerate(ORDER)
            if slot == s and item[0] == "apply" and item in BY_ACT))
        masked_done = counted("masked_done", unit_counts)
        hi_dve = counted("hi_dve", lambda s: unit_counts(s, lambda u: not hi_by_act(u)))
        dense_lo = counted("dense_lo", lambda s: item_counts("job", s))
        elu_min = counted("elu_min", lambda s: item_counts("elu_min", s))
        shifted = counted("shifted", lambda s: item_counts("shift", s))
        ffn_input = counted("ffn_input", lambda s: counts(
            ((), place, late) for place, (item, slot, late) in enumerate(ORDER) if slot == s and item == ("apply", 1)))
        dve_chain = counted("dve_chain", lambda s: link_counts(s, links))
        lo_done = counted("lo_done", unit_counts)
        affine_done = counted("affine_done", lambda s: item_counts("affine", s))
        x_loaded = [sem(f"x_loaded{s}") for s in S2]
        stacked = [sem(f"stacked{s}") for s in S2]
        out_stored = [sem(f"out_stored{s}") for s in S2]
        OUT_CREDIT = 16
        STACK_DMAS = len(STACK) * (P // D1)
        transposed = [[sem(f"transposed{s}_{i}") for i in range(TRING)] for s in S2]
        SLOT_UNITS = [[u for u in range(len(UNITS)) if UNITS[u][1] == s] for s in S2]
        LATE_UNITS = [sum(UNITS[u][4] for u in SLOT_UNITS[s]) for s in S2]
        assert all(len(own_units) % TRING == 0 for own_units in SLOT_UNITS)

        w_loaded = sem("w_loaded")
        ident_ready = sem("ident_ready")
        setup_pool = sem("setup_pool")
        setup_dve = sem("setup_dve")
        setup_pe = sem("setup_pe")
        dve_setup_chain = sem("dve_setup_chain")
        masking = sem("masking")
        split_seen = sem("split_seen")
        trans_free_seen = sem("trans_free_seen")
        credit_cell = sb("credit_cell", [P, 32])
        credit_dma = sb("credit_dma", [1, 16 * SLOTS])
        credit_dve = sb("credit_dve", [P, 16])

        stage_w = {k: buf[0][:, CT * half:CT * half + CT, :]
                   for buf, keys in ((xcur, ("h0", "q")), (xout, ("k", "v")), (za, ("f1", "f2")), (zb, ("h2", "h3")))
                   for half, k in enumerate(keys)}
        stage_d1 = zb[1][:, 0:CT, :]
        stage_d2 = zb[1][:, CT:2 * CT, :]
        stage_t1 = za[1][:, 0:CT, :]
        stage_t2 = za[1][:, CT:2 * CT, :]
        stage_g = xcur[1][:, 0:CT, :]
        stage_s0 = xcur[1][:, CT, :].rearrange("p (t n) -> p t n", t=CT)
        stage_s2 = xcur[1][:, CT + 1, :].rearrange("p (t n) -> p t n", t=CT)
        stage_a0 = xout[1][:, 0:2, :]
        stage_a2 = xout[1][:, 2, 0:C // 2]
        stage_scratch = xout[1][:, 3, :]
        stage_adj = masked_r[:, :, :].bitcast(i32)
        stage_flag = prob_r

        NORM_SRC = {0: za, 1: za, 2: za, 3: za, "ffn": za, "out1": zb}
        NORM_DST = {0: xcur, 1: xout, 2: xcur, 3: xout, "ffn": zb, "out1": xcur}
        VAR, PRODUCT, RATIO, Y, SHIFT = range(5)

        block = ctx.enter_context(nc.Block())

        def wait(eng, it, here, counter, slot, key):
            semaphore, table, _ = counter[slot]
            place, n, _ = table[key]
            if place > here:
                n -= len(table)
            eng.wait_ge(semaphore, it * len(table) + (n + CREDIT[slot]))

        def wait_unit(eng, it, here, counter, u):
            wait(eng, it, here, counter, UNITS[u][1], u)

        def last_user(it, active, u, depth):
            v = u - depth
            while v >= 0 and not active(UNITS[v][4]):
                v -= depth
            if v < 0 and isinstance(it, int) and it == 0:
                return None
            return v % len(UNITS)

        def wait_user(eng, it, here, active, counter, u, depth):
            v = last_user(it, active, u, depth)
            if v is not None:
                wait_unit(eng, it, here, counter, v)

        def transposed_by(u):
            s = UNITS[u][1]
            return transposed[s][SLOT_UNITS[s].index(u) % TRING]

        def wait_transposed(eng, it, here, u):
            s = UNITS[u][1]
            n = SLOT_UNITS[s].index(u)
            missing = len([m for m in range(LATE_UNITS[s]) if m % TRING == n % TRING])
            count = n // TRING + 1 - missing
            if STEP_PLACE[u] > here:
                count -= len(SLOT_UNITS[s]) // TRING
            eng.wait_ge(transposed_by(u), it * (16 * len(SLOT_UNITS[s]) // TRING) + 16 * count)

        def wait_hi(eng, it, here, u):
            wait_unit(eng, it, here, hi_act if hi_by_act(u) else hi_dve, u)

        def turns(eng, run):
            run(0, lambda late: not late)
            with eng.Fori(1, TURNS) as it:
                run(it, lambda late: True)
            run(TURNS, lambda late: late)

        def wait_split_free(eng, it, here, active, u):
            v = last_user(it, active, u, TRING)
            if v is not None:
                wait_transposed(eng, it, here, v)

        def stages(item):
            return [pipe[item[1] - lag] if item[1] >= lag else None for lag in (0, LAG_HI, LAG_T, LAG_PV)]

        def graph(it, late):
            return it - 1 if late else it

        def everywhere(key):
            return rows[key][:].unsqueeze(1).broadcast_to([P, NB, C])

        def w_view(w):
            return w.rearrange("(t p) n -> p t n", p=P)

        @block.sync
        def _(sp):
            for k, src in (("h0", gat_w), ("q", w_qkv[:, 0:C]), ("k", w_qkv[:, C:2 * C]), ("v", w_qkv[:, 2 * C:3 * C]),
                           ("f1", ffn_w1), ("f2", ffn_w2), ("h2", mh_w), ("h3", dot_w3)):
                sp.dma_start(stage_w[k], w_view(src)).then_inc(w_loaded, 16)
            sp.dma_start(stage_d1, w_view(dot_w1)).then_inc(w_loaded, 16)
            sp.dma_start(stage_d2, w_view(dot_w2)).then_inc(w_loaded, 16)
            for k, src in (("g1", ln1_g), ("b1", ln1_b), ("g2", ln2_g), ("b2", ln2_b), ("fb2", ffn_b2)):
                sp.dma_start(rows[k][:], src.rearrange("(o n) -> o n", o=1).broadcast_to([P, C])).then_inc(w_loaded, 16)
            sp.dma_start(ffn_bias[:], ffn_b1.rearrange("(t p) -> p t", p=P), allow_slow_non_contiguous=True).then_inc(w_loaded, 16)
            sp.dma_start(stage_a0, gat_a.rearrange("(t n) o -> o t n", t=2).broadcast_to([P, 2, C])).then_inc(w_loaded, 16)
            sp.dma_start(stage_a2, mh_a.rearrange("(o n) -> o n", o=1).broadcast_to([P, C // 2])).then_inc(w_loaded, 16)
            sp.dma_start(stage_adj, adj.rearrange("(b p) n -> p b n", p=P)).then_inc(w_loaded, 16)

            def load_x(g, s):
                sp.dma_start(xin[s][:], x[g * SLOTS + s].rearrange("(b p) c -> p b c", p=P)).then_inc(x_loaded[s], 16)

            for s in S2:
                sp.dma_start(credit_dma[:, 16 * s:16 * s + 16], ln1_g[0:16].rearrange("(o n) -> o n", o=1)).then_inc(out_stored[s], OUT_CREDIT)
                load_x(0, s)

            def run(it, active):
                for here, (item, s, late) in enumerate(ORDER):
                    if item[0] == "step":
                        u = stages(item)[2]
                        if u is not None and active(UNITS[u][4]):
                            wait_unit(sp, it, here, lo_done, u)
                            sp.sem_inc(split_seen, 1)
                            if last_user(it, active, u, TRING) is not None:
                                wait_user(sp, it, here, active, values_done, u, TRING)
                                sp.sem_inc(trans_free_seen, 1)
                            sp.dma_start_transpose(
                                trans_r[:, u % TRING].rearrange("p a b n -> p (a b) n"),
                                split_r[:, u % TRING].rearrange("p a n -> p (a n)")).then_inc(transposed_by(u), 16)
                    if not active(late):
                        continue
                    g = graph(it, late)
                    if item[0] == "load":
                        if not (isinstance(g, int) and g + 1 == TURNS):
                            wait(sp, it, here, applied, s, (0,))
                            load_x(g + 1, s)
                    elif item[0] == "stack":
                        j = GROUPS[GROUP_OF[1]].index(("k", CT - 1))
                        wait(sp, it, here, dense_lo, s, (GROUP_OF[1], j))
                        for h in range(P // D1):
                            for c, (q_part, k_part) in enumerate(STACK):
                                pair = slice(q_part, 3 + k_part, 2 + k_part - q_part)
                                sp.dma_start(stack[s][c * D1:(c + 1) * D1, h, :, :, :],
                                             qk[s][h * D1:(h + 1) * D1, pair, :, :]).then_inc(stacked[s], 16)
                    elif item[0] == "store":
                        wait(sp, it, here, applied, s, (3,))
                        sp.dma_start(out[g * SLOTS + s].rearrange("(b p) c -> p b c", p=P), xout[s][:]).then_inc(out_stored[s], 16)

            run(0, lambda late: not late)
            with sp.Fori(1, TURNS - 1) as it:
                run(it, lambda late: True)
            run(TURNS - 1, lambda late: True)
            run(TURNS, lambda late: late)
            for s in S2:
                sp.wait_ge(out_stored[s], 16 * TURNS + OUT_CREDIT)

        @block.gpsimd
        def _(pool):
            nc.gpsimd.memset(ident32[:], 0.0).then_inc(setup_pool, 1)
            nc.gpsimd.memset(sel_row[:], 0.0).then_inc(setup_pool, 1)
            nc.gpsimd.memset(sel_col[:], 0.0).then_inc(setup_pool, 1)
            pool.wait_ge(setup_pool, 3)
            nc.gpsimd.affine_select(out=ident32[:], in_=ident32[:], compare_op=ALU.not_equal, fill=1.0, base=0,
                                    pattern=[[-1, P]], channel_multiplier=1).then_inc(ident_ready, 1)
            for n, (tile, at_row) in enumerate(((sel_row, 0), (sel_row, 32), (sel_col, 64), (sel_col, 96))):
                width = tile.shape[2]
                nc.gpsimd.affine_select(out=tile[:], in_=tile[:], compare_op=ALU.not_equal, fill=1.0,
                                        base=-at_row, pattern=[[-1, HEADS[2]], [0, width]],
                                        channel_multiplier=1).then_inc(setup_pool, 1)
                pool.wait_ge(setup_pool, 4 + n)
            for n, (semaphore, _, start) in enumerate([*lo_done, *affine_done]):
                nc.gpsimd.memset(credit_cell[:, 2 + n:3 + n], 0.0).then_inc(semaphore, start)

            def run(it, active):
                for here, (item, s, late) in enumerate(ORDER):
                    if item[0] == "step":
                        u = stages(item)[1]
                        if u is not None and active(UNITS[u][4]):
                            wait_hi(pool, it, here, u)
                            nc.gpsimd.tensor_tensor(split_r[:, u % TRING, 1, :], prob_r[:, u % RING, :],
                                                    split_r[:, u % TRING, 0, :], ALU.subtract).then_inc(lo_done[UNITS[u][1]][0], 1)
                    elif item[0] == "affine" and active(late):
                        if item[1] == 1:
                            wait(pool, it, here, ffn_input, s, ())
                            ins = nc.gpsimd.tensor_tensor(zb[s][:], xout[s][:], everywhere("fb2"), ALU.add)
                        else:
                            wait(pool, it, here, ffn_input, s, ())
                            ins = nc.gpsimd.tensor_tensor(xcur[s][:], xcur[s][:], everywhere("b2"), ALU.add)
                        ins.then_inc(affine_done[s][0], 1)

            turns(pool, run)

        @block.scalar
        def _(act):
            act.wait_ge(ident_ready, 1)
            for n, (semaphore, _, start) in enumerate([*relu_done, *probs_done, *hi_act, *dense_hi, *elu_exp, *divided, *applied]):
                nc.scalar.copy(credit_cell[:, 8 + n:9 + n], ident32[:, 0:1]).then_inc(semaphore, start)

            def dense(it, here, g, j, s):
                kind, n = GROUPS[g][j]
                bank = acc_ps[s][:, 2 * (j % 2):2 * (j % 2) + 2, :].rearrange("p a c -> p (a c)")
                wait(act, it, here, dense_full, s, (g, j))
                if kind == "xt":
                    ins = nc.scalar.copy(xt[s][:, 0, n, :], bank)
                elif kind in ("q", "k", "g"):
                    dst = proj_k if kind == "k" else proj
                    scale = {"q": QK_SCALE, "k": 1.0, "g": SLOPE}[kind] / WSCALE
                    ins = nc.scalar.activation(dst[s][:, 0, n, :], bank, ACT.Copy, scale=scale)
                elif kind in ("s0", "s2"):
                    ins = nc.scalar.activation(s12[s][:], bank, ACT.Copy, scale=1.0 / WSCALE)
                elif kind == "f1":
                    ins = nc.scalar.activation(za[s][:, 2 * n:2 * n + 2, :].rearrange("p a c -> p (a c)"), bank,
                                               ACT.Relu, bias=ffn_bias[:, n:n + 1], scale=1.0 / WSCALE)
                elif kind == "f2":
                    ins = nc.scalar.activation(za[s][:, 2 * n:2 * n + 2, :].rearrange("p a c -> p (a c)"), bank,
                                               ACT.Copy, scale=1.0 / WSCALE)
                else:
                    ins = nc.scalar.activation(val[s][:, 0, 2 * n:2 * n + 2, :].rearrange("p a c -> p (a c)"), bank,
                                               ACT.Copy, scale=1.0 / WSCALE)
                ins.then_inc(dense_hi[s][0], 1)

            def relu(it, here, active, u):
                wait_unit(act, it, here, scores_done, u)
                wait_user(act, it, here, active, masked_done, u, RING)
                nc.scalar.activation(relu_r[:, u % RING, :], scores_ps[u % RING][:], ACT.Relu,
                                     scale=1.0 / SLOPE - 1.0).then_inc(relu_done[UNITS[u][1]][0], 1)

            def probs(it, here, active, u):
                layer, s, h, b, _ = UNITS[u]
                wait_unit(act, it, here, masked_done, u)
                wait_user(act, it, here, active, lo_done, u, RING)
                nc.scalar.activation(prob_r[:, u % RING, :], masked_r[:, u % RING, :], ACT.Exp,
                                     bias=low_r[:, u % RING:u % RING + 1], scale=-1.0,
                                     accum_out=rowsum[s][:, b, h:h + 1]).then_inc(probs_done[s][0], 1)

            def run(it, active):
                for here, (item, s, late) in enumerate(ORDER):
                    if item[0] == "step":
                        new, middle, _, _ = stages(item)
                        p = pipe[item[1] - LAG_P] if item[1] >= LAG_P else None
                        if new is not None and active(UNITS[new][4]) and LEAKY[UNITS[new][0]]:
                            relu(it, here, active, new)
                        if p is not None and active(UNITS[p][4]):
                            probs(it, here, active, p)
                        if middle is not None and active(UNITS[middle][4]) and hi_by_act(middle):
                            u = middle
                            wait_unit(act, it, here, probs_done, u)
                            wait_split_free(act, it, here, active, u)
                            nc.scalar.copy(split_r[:, u % TRING, 0, :], prob_r[:, u % RING, :]).then_inc(hi_act[UNITS[u][1]][0], 1)
                    elif not active(late):
                        continue
                    elif item[0] == "job":
                        dense(it, here, item[1], item[2], s)
                    elif item[0] == "elu_min":
                        wait(act, it, here, elu_min, s, item[1:])
                        nc.scalar.activation(zb[s][:], zb[s][:], ACT.Exp).then_inc(elu_exp[s][0], 1)
                    elif item in BY_ACT and item[0] == "divide":
                        recip = next(place for place, (other, slot, _) in enumerate(ORDER)
                                     if slot == s and other == ("recip", item[1]))
                        wait(act, it, here, dve_chain, s, (recip, 0))
                        for b in range(NB):
                            scale = rinv[s][:, b, 0:1]
                            ins = nc.scalar.activation(za[s][:, b, :], acc_ps[s][:, b, :], ACT.Relu, scale=scale)
                            if item[1] == 0:
                                ins = nc.scalar.activation(zb[s][:, b, :], acc_ps[s][:, b, :], ACT.Exp, scale=scale)
                        ins.then_inc(divided[s][0], 1)
                    elif item in BY_ACT:
                        which = item[1]
                        wait(act, it, here, shifted, s, (which,))
                        for b in range(NB):
                            ins = nc.scalar.activation(NORM_DST[which][s][:, b, :], NORM_SRC[which][s][:, b, :], ACT.Identity,
                                                       bias=small[s][:, SHIFT, b:b + 1], scale=small[s][:, Y, b:b + 1])
                        ins.then_inc(applied[s][0], 1)

            turns(act, run)

        @block.vector
        def _(dve):
            setup = [0]

            def after(ins):
                setup[0] += 1
                ins.then_inc(dve_setup_chain, 1)
                dve.wait_ge(dve_setup_chain, setup[0])

            for n, (semaphore, _, start) in enumerate([*masked_done, *hi_dve, *dense_lo, *elu_min, *shifted, *ffn_input,
                                                       *dve_chain]):
                nc.vector.memset(credit_dve[:, n:n + 1], 0.0).then_inc(semaphore, start)
            dve.wait_ge(w_loaded, 16 * 19)
            dve.wait_ge(ident_ready, 1)
            after(nc.vector.tensor_copy(identb[:], ident32[:]))
            after(nc.vector.tensor_scalar(stage_flag[:], stage_adj, 0.0, 1.0, ALU.is_gt, ALU.subtract))
            after(nc.vector.tensor_scalar(neg_mask[:], stage_flag[:], MASKED, None, ALU.mult))

            def split_weight(dst, src, scale):
                after(nc.vector.tensor_scalar(dst[:, 0], src, scale, None, ALU.mult))
                after(nc.vector.scalar_tensor_tensor(out=dst[:, 1], in0=src, scalar=scale, in1=dst[:, 0],
                                                     op0=ALU.mult, op1=ALU.subtract))

            for key, stage_s, heads, stage_src in (("s0", stage_s0, 1, stage_w["h0"]), ("s2", stage_s2, HEADS[2], stage_w["h2"])):
                after(nc.vector.memset(stage_s, 0.0))
                width = C // heads
                for h in range(heads):
                    for side in range(2):
                        for t in range(CT):
                            a = stage_a0[:, side, :] if heads == 1 else stage_a2[:, side * width:(side + 1) * width]
                            col = 64 * side + h
                            after(nc.vector.tensor_tensor_reduce(
                                out=stage_scratch[:, 0:width], in0=stage_src[:, t, h * width:(h + 1) * width], in1=a,
                                scale=1.0, scalar=0.0, op0=ALU.mult, op1=ALU.add, accum_out=stage_s[:, t, col:col + 1]))
                for side in range(2):
                    after(nc.vector.tensor_copy(stage_s[:, :, 64 * side + 32:64 * side + 32 + heads],
                                                stage_s[:, :, 64 * side:64 * side + heads]))
                split_weight(W[key], stage_s, WSCALE * SLOPE)
            for k in ("h0", "q", "k", "v", "f1", "f2", "h2", "h3"):
                split_weight(W[k], stage_w[k], WSCALE)
            dve.wait_ge(setup_pe, 1)
            nc.vector.tensor_copy(stage_t1, acc_ps[0][:, 0:2, :])
            nc.vector.tensor_copy(stage_t2, acc_ps[0][:, 2:4, :]).then_inc(setup_dve, 1)
            dve.wait_ge(setup_pe, 2)
            after(nc.vector.tensor_copy(stage_g, acc_ps[1][:, 0:2, :]))
            split_weight(W["g"], stage_g, WSCALE)
            nc.vector.memset(credit_dve[:, 15:16], 0.0).then_inc(setup_dve, 1)

            done_links = [0] * SLOTS

            def link(s, ins):
                done_links[s] += 1
                ins.then_inc(dve_chain[s][0], 1)

            def own(it, s):
                semaphore, table, _ = dve_chain[s]
                dve.wait_ge(semaphore, it * len(table) + (done_links[s] + CREDIT[s]))

            def dense(it, here, g, j, s):
                kind, n = GROUPS[g][j]
                bank = acc_ps[s][:, 2 * (j % 2):2 * (j % 2) + 2, :].rearrange("p a c -> p (a c)")
                wait(dve, it, here, dense_hi, s, (g, j))

                def lo(dst, hi, scale):
                    return nc.vector.scalar_tensor_tensor(out=dst, in0=bank, scalar=scale, in1=hi,
                                                          op0=ALU.mult, op1=ALU.subtract)

                if kind == "xt":
                    ins = lo(xt[s][:, 1, n, :], xt[s][:, 0, n, :], 1.0)
                elif kind in ("q", "k", "g"):
                    dst = proj_k if kind == "k" else proj
                    scale = {"q": QK_SCALE, "k": 1.0, "g": SLOPE}[kind] / WSCALE
                    ins = lo(dst[s][:, 1, n, :], dst[s][:, 0, n, :], scale)
                elif kind in ("s0", "s2"):
                    for quadrant in (1, 3):
                        r = slice(32 * quadrant, 32 * quadrant + 32)
                        ins = nc.vector.scalar_tensor_tensor(out=s12[s][r, :], in0=bank[r, :], scalar=1.0 / WSCALE,
                                                             in1=s12[s][r, :], op0=ALU.mult, op1=ALU.subtract)
                elif kind == "f1":
                    hid = za[s][:, 2 * n:2 * n + 2, :].rearrange("p a c -> p (a c)")
                    link(s, nc.vector.tensor_copy(proj[s][:, 0, n, :], hid))
                    own(it, s)
                    ins = nc.vector.tensor_tensor(proj[s][:, 1, n, :], hid, proj[s][:, 0, n, :], ALU.subtract)
                elif kind == "f2":
                    wait(dve, it, here, affine_done, s, (1,))
                    ins = nc.vector.tensor_tensor(za[s][:, 2 * n:2 * n + 2, :], za[s][:, 2 * n:2 * n + 2, :],
                                                  zb[s][:, 2 * n:2 * n + 2, :], ALU.add)
                else:
                    v = [val[s][:, p, 2 * n:2 * n + 2, :].rearrange("p a c -> p (a c)") for p in range(2)]
                    ins = lo(v[1], v[0], 1.0 / WSCALE)
                ins.then_inc(dense_lo[s][0], 1)

            def finish(it, here, item, s, late):
                kind = item[0]
                col = [small[s][:, n, :] for n in range(5)]
                if kind == "recip":
                    heads = HEADS[item[1]]
                    last = max(u for u in SLOT_UNITS[s] if UNITS[u][0] == item[1])
                    wait(dve, it, here, values_done, s, last)
                    link(s, nc.vector.reciprocal(rinv[s][:, :, 0:heads], rowsum[s][:, :, 0:heads]))
                elif kind == "divide":
                    heads = HEADS[item[1]]
                    own(it, s)
                    link(s, nc.vector.tensor_tensor(
                        za[s][:].rearrange("p b (h d) -> p b h d", h=heads),
                        acc_ps[s][:].rearrange("p b (h d) -> p b h d", h=heads),
                        rinv[s][:, :, 0:heads].unsqueeze(3).broadcast_to([P, NB, heads, C // heads]), ALU.mult))
                elif kind == "elu_min":
                    own(it, s)
                    nc.vector.tensor_scalar(zb[s][:], za[s][:], 0.0, None, ALU.min).then_inc(elu_min[s][0], 1)
                    link(s, nc.vector.scalar_tensor_tensor(out=za[s][:], in0=za[s][:], scalar=0.0, in1=xcur[s][:],
                                                           op0=ALU.max, op1=ALU.add))
                elif kind == "elu_sum":
                    wait(dve, it, here, divided, s, (item[1],))
                    link(s, nc.vector.scalar_tensor_tensor(out=za[s][:], in0=zb[s][:], scalar=1.0, in1=za[s][:],
                                                           op0=ALU.min, op1=ALU.add))
                elif kind == "elu_add":
                    own(it, s)
                    if item[1] == 0:
                        dve.wait_ge(x_loaded[s], graph(it, late) * 16 + 16)
                        terms = (za, xin)
                    else:
                        wait(dve, it, here, elu_exp, s, (item[1],))
                        terms = (zb, za)
                    link(s, nc.vector.scalar_tensor_tensor(out=za[s][:], in0=terms[0][s][:], scalar=-1.0, in1=terms[1][s][:],
                                                           op0=ALU.add, op1=ALU.add))
                elif kind == "residual":
                    if item[1] == 3:
                        wait(dve, it, here, divided, s, (3,))
                    else:
                        own(it, s)
                    link(s, nc.vector.tensor_tensor(za[s][:], za[s][:], xcur[s][:], ALU.add))
                elif kind == "stats":
                    _, b, which = item
                    if b == 0 and which == "ffn":
                        wait(dve, it, here, dense_lo, s, (FFN, len(GROUPS[FFN]) - 1))
                    elif b == 0:
                        own(it, s)
                    link(s, nc.vector.bn_stats(stats[s][:, b, :], NORM_SRC[which][s][:, b, :]))
                elif kind == "aggregate":
                    own(it, s)
                    dve.sem_inc(masking, 1)
                    for b in range(NB):
                        ins = nc.vector.bn_aggr(moments[s][:, b, :], stats[s][:, b, :])
                    link(s, ins)
                elif kind == "add_eps":
                    own(it, s)
                    link(s, nc.vector.tensor_scalar(col[VAR], moments[s][:, :, 1], EPS, None, ALU.add))
                elif kind == "seed":
                    own(it, s)
                    link(s, nc.vector.tensor_scalar(col[Y].bitcast(i32), col[VAR].bitcast(i32), -0.5, RSQRT_SEED,
                                                    ALU.mult, ALU.add))
                elif kind == "product":
                    own(it, s)
                    link(s, nc.vector.tensor_tensor(col[PRODUCT], col[VAR], col[Y], ALU.mult))
                elif kind == "newton":
                    _, n, part, _ = item
                    own(it, s)
                    if part == 0:
                        ins = nc.vector.scalar_tensor_tensor(out=col[RATIO], in0=col[PRODUCT], scalar=-0.5, in1=col[Y],
                                                             op0=ALU.mult, op1=ALU.mult)
                    else:
                        for c in (PRODUCT, Y) if n < 2 else (Y,):
                            ins = nc.vector.scalar_tensor_tensor(out=col[c], in0=col[RATIO], scalar=1.5, in1=col[c],
                                                                 op0=ALU.add, op1=ALU.mult)
                    link(s, ins)
                elif kind == "shift":
                    own(it, s)
                    nc.vector.scalar_tensor_tensor(out=col[SHIFT], in0=moments[s][:, :, 0], scalar=-1.0, in1=col[Y],
                                                   op0=ALU.mult, op1=ALU.mult).then_inc(shifted[s][0], 1)
                elif kind == "gain":
                    which = item[1]
                    own(it, s)
                    for b in range(NB):
                        ins = nc.vector.scalar_tensor_tensor(
                            out=zb[s][:, b, :], in0=za[s][:, b, :], scalar=moments[s][:, b, 0:1],
                            in1=rows[{1: "g1", "ffn": "g2"}[which]][:], op0=ALU.subtract, op1=ALU.mult)
                    link(s, ins)
                elif kind == "apply":
                    which = item[1]
                    own(it, s)
                    if which == 1:
                        dve.wait_ge(out_stored[s], graph(it, late) * 16 + OUT_CREDIT)
                    if which == "ffn":
                        wait(dve, it, here, affine_done, s, (2,))
                    for b in range(NB):
                        added = rows["b1"][:] if which == 1 else xcur[s][:, b, :]
                        ins = nc.vector.scalar_tensor_tensor(
                            out=NORM_DST[which][s][:, b, :], in0=zb[s][:, b, :], scalar=small[s][:, Y, b:b + 1], in1=added,
                            op0=ALU.mult, op1=ALU.add)
                    if which == 1:
                        ins.then_inc(ffn_input[s][0], 1)
                    else:
                        link(s, ins)

            def masked(it, here, active, u):
                layer, s, h, b, _ = UNITS[u]
                wait_user(dve, it, here, active, probs_done, u, RING)
                if LEAKY[layer]:
                    wait(dve, it, here, relu_done, s, u)
                    second = relu_r[:, u % RING, :]
                else:
                    wait(dve, it, here, scores_done, s, u)
                    second = neg_mask[:, b, :]
                dve.sem_inc(masking, 1)
                nc.vector.tensor_tensor_reduce(out=masked_r[:, u % RING, :], in0=scores_ps[u % RING][:], in1=second,
                                               scale=-1.0, scalar=BIG, op0=ALU.add, op1=ALU.min,
                                               accum_out=low_r[:, u % RING:u % RING + 1]).then_inc(masked_done[s][0], 1)

            def run(it, active):
                for s in S2:
                    done_links[s] = 0
                for here, (item, s, late) in enumerate(ORDER):
                    if item[0] == "step":
                        new, middle, _, _ = stages(item)
                        if new is not None and active(UNITS[new][4]):
                            masked(it, here, active, new)
                        if middle is not None and active(UNITS[middle][4]) and not hi_by_act(middle):
                            u = middle
                            wait_unit(dve, it, here, probs_done, u)
                            wait_split_free(dve, it, here, active, u)
                            nc.vector.tensor_copy(split_r[:, u % TRING, 0, :], prob_r[:, u % RING, :]).then_inc(hi_dve[UNITS[u][1]][0], 1)
                    elif not active(late):
                        done_links[s] += links(item)
                    elif item[0] == "job":
                        dense(it, here, item[1], item[2], s)
                    elif item not in BY_ACT:
                        before = done_links[s]
                        finish(it, here, item, s, late)
                        assert done_links[s] == before + links(item)

            turns(dve, run)

        @block.tensor
        def _(pe):
            pe.wait_ge(ident_ready, 1)
            pe.wait_ge(w_loaded, 16 * 19)
            for half, src in enumerate((stage_d1, stage_d2)):
                for tf in range(CT):
                    for tc in range(CT):
                        ins = nc.tensor.transpose(acc_ps[0][:, 2 * half + tf, tc * P:(tc + 1) * P],
                                                  src[:, tc, tf * P:(tf + 1) * P], ident32[:])
            ins.then_inc(setup_pe, 1)
            pe.wait_ge(setup_dve, 1)
            for tc in range(CT):
                for tf in range(CT):
                    ins = nc.tensor.matmul(acc_ps[1][:, tc, :], stage_t1[:, tf, tc * P:(tc + 1) * P], stage_t2[:, tf, :],
                                           start=(tf == 0), stop=(tf == CT - 1))
            ins.then_inc(setup_pe, 1)
            for semaphore, _, start in [*scores_done, *values_done, *dense_full]:
                nc.tensor.transpose(scores_ps[0][:, 0:P], ident32[:], ident32[:]).then_inc(semaphore, start)
            pe.wait_ge(setup_dve, 2)
            pe.wait_ge(setup_pool, 7)

            TERMS = [(0, 0), (0, 1), (1, 0)]

            def dense(it, here, g, j, s, late):
                kind, n = GROUPS[g][j]
                bank = acc_ps[s][:, 2 * (j % 2):2 * (j % 2) + 2, :]
                flat = bank.rearrange("p a c -> p (a c)")
                if j == 0:
                    if g == 0:
                        pe.wait_ge(x_loaded[s], graph(it, late) * 16 + 16)
                        wait(pe, it, here, applied, s, (3,))
                    elif g == FFN:
                        wait(pe, it, here, ffn_input, s, ())
                    else:
                        wait(pe, it, here, applied, s, ({1: 0, 3: "out1", 4: 2}[g],))
                if j >= 2:
                    wait(pe, it, here, dense_lo, s, (g, j - 2))
                if j == 2 or (kind == "f2" and n == 0):
                    wait(pe, it, here, dense_lo, s, (g, j - 1))
                if kind == "xt":
                    src = {0: xin, FFN: xout}.get(g, xcur)
                    for b in range(NB):
                        ins = nc.tensor.transpose(flat[:, b * P:(b + 1) * P], src[s][:, b, n * P:(n + 1) * P], ident32[:])
                elif kind in ("q", "k", "g", "s0", "s2", "f1"):
                    ops = [(wp, xp, t) for t in range(CT) for wp, xp in TERMS]
                    for i, (wp, xp, t) in enumerate(ops):
                        ins = nc.tensor.matmul(flat, W[kind][:, wp, t, n * P:(n + 1) * P], xt[s][:, xp, t, :],
                                               start=(i == 0), stop=(i == len(ops) - 1))
                else:
                    left = proj if kind == "f2" else xt
                    ops = [(xp, wp, t) for t in range(CT) for xp, wp in TERMS]
                    for half in range(2):
                        b = 2 * n + half
                        for i, (xp, wp, t) in enumerate(ops):
                            ins = nc.tensor.matmul(bank[:, half, :], left[s][:, xp, t, b * P:(b + 1) * P],
                                                   W[kind][:, wp, t, :], start=(i == 0), stop=(i == len(ops) - 1))
                ins.then_inc(dense_full[s][0], 1)

            def scores(it, here, active, u):
                layer, s, h, b, late = UNITS[u]
                ps = scores_ps[u % RING][:]
                q = slice(b * P, (b + 1) * P)
                if h == 0 and b == 0:
                    g = GROUP_OF[layer]
                    wait(pe, it, here, dense_lo, s, (g, len(GROUPS[g]) - 1))
                    if layer == 1:
                        pe.wait_ge(stacked[s], graph(it, late) * (16 * STACK_DMAS) + 16 * STACK_DMAS)
                wait_user(pe, it, here, active, masked_done, u, RING)
                if layer == 1:
                    t, hq = divmod(h, P // D1)
                    ops = [(stack[s][:, hq, 0, t, q], stack[s][:, hq, 1, t, :])]
                elif layer == 3:
                    ops = [(proj[s][:, gp, t, q], xt[s][:, xp, t, :]) for t in range(CT) for gp, xp in TERMS]
                else:
                    ops = [(s12[s][:, q], sel_row[:, h, :]), (sel_col[:, h, :], s12[s][:])]
                if layer != 1:
                    ops.append((identb[:], neg_mask[:, b, :]))
                for i, (left, right) in enumerate(ops):
                    ins = nc.tensor.matmul(ps, left, right, start=(i == 0), stop=(i == len(ops) - 1))
                ins.then_inc(scores_done[s][0], 1)

            def values(it, here, u):
                layer, s, h, b, _ = UNITS[u]
                width = C // HEADS[layer]
                cols = slice(h * width, (h + 1) * width)
                wait_transposed(pe, it, here, u)
                ops = [(pp, vp, jb) for jb in range(NB) for pp, vp in TERMS]
                for i, (pp, vp, jb) in enumerate(ops):
                    ins = nc.tensor.matmul(acc_ps[s][:, b, cols], trans_r[:, u % TRING, pp, jb, :], val[s][:, vp, jb, cols],
                                           start=(i == 0), stop=(i == len(ops) - 1))
                ins.then_inc(values_done[s][0], 1)

            def run(it, active):
                for here, (item, s, late) in enumerate(ORDER):
                    if item[0] == "step":
                        new, _, _, oldest = stages(item)
                        if new is not None and active(UNITS[new][4]):
                            scores(it, here, active, new)
                        if oldest is not None and active(UNITS[oldest][4]):
                            values(it, here, oldest)
                    elif item[0] == "job" and active(late):
                        dense(it, here, item[1], item[2], s, late)

            turns(pe, run)


_INS = ['x', 'adj', 'L0_gnn_W', 'L0_gnn_a', 'L1_gnn_w_qkv', 'L1_gnn_ln1_g', 'L1_gnn_ln1_b', 'L1_gnn_ln2_g',
        'L1_gnn_ln2_b', 'L1_gnn_w1', 'L1_gnn_b1', 'L1_gnn_w2', 'L1_gnn_b2', 'L2_gnn_W', 'L2_gnn_a',
        'L3_gnn_W1', 'L3_gnn_W2', 'L3_gnn_W3']
_OUT = ((32, 512, 256), 'float32')


def kernel(**inputs):
    import numpy as _np
    import concourse.bacc as _bacc
    from concourse import mybir as _mybir
    from concourse.bass_utils import run_bass_kernel_spmd as _run

    nc = _bacc.Bacc("TRN2", target_bir_lowering=False, num_devices=1)
    arrays, args = {}, []
    for name in _INS:
        a = _np.ascontiguousarray(inputs[name])
        arrays[f"in_{name}_dram"] = a
        args.append(nc.dram_tensor(f"in_{name}_dram", a.shape, _mybir.dt.from_np(a.dtype), kind="ExternalInput").ap())
    shape, dtype = _OUT
    args.append(nc.dram_tensor("out_dram", shape, _mybir.dt.from_np(_np.dtype(dtype)), kind="ExternalOutput").ap())
    graph_layers_kernel(nc, *args)
    r = _run(nc, [arrays], core_ids=[0])
    return r.results[0]["out_dram"]
```
